# Optimizing a Trainium2 kernel written in Bass

```python
import numpy as np
import jax
import jax.numpy as jnp

def _softmax(x, axis=-1):
    return jax.nn.softmax(x, axis=axis)

def _gelu(x):
    return jax.nn.gelu(x, approximate=True)

def _silu(x):
    return jax.nn.silu(x)

def _sigmoid(x):
    return jax.nn.sigmoid(x)

def _layernorm(x, axis=-1, eps=1e-05):
    m = jnp.mean(x, axis=axis, keepdims=True)
    v = jnp.var(x, axis=axis, keepdims=True)
    return (x - m) / jnp.sqrt(v + eps)

def _scatter_add(tgt, idx, src, axis=0):
    return tgt.at[idx].add(src)

def _segment_sum(src, seg, n):
    return jax.ops.segment_sum(src, seg, n)
kernel_name = 'mk_seq_preln_d1_jaxref_r8_34f60e'

def setup_inputs(seed: int=0):
    np.random.seed(seed)
    _w = jnp.asarray

    def _L0_attn_setup():
        import jax, jax.numpy as jnp
        import numpy as np
        EPS = 1e-05
        NUM_HEADS = 16
        FEATURE_DIM = 16
        CHUNK = 64

        def _phi(x):
            f = x.shape[-1]
            return (x[..., :, None] * x[..., None, :]).reshape(*x.shape[:-1], f * f)
        key = jax.random.key(seed)
        ks = jax.random.split(key, 5)
        b, l, d = (4, 256, 128)
        h, f = (NUM_HEADS, FEATURE_DIM)
        hd = d // h
        scale = 0.02
        return {'hidden_states': jax.random.normal(ks[0], (b, l, d), jnp.float32), 'Wq': jax.random.normal(ks[1], (d, h * f), jnp.float32) * scale, 'Wk': jax.random.normal(ks[2], (d, h * f), jnp.float32) * scale, 'Wv': jax.random.normal(ks[3], (d, h * hd), jnp.float32) * scale, 'Wo': jax.random.normal(ks[4], (h * hd, d), jnp.float32) * scale}
    _L0_attn_in = _L0_attn_setup()

    def _L0_ffn_setup():
        import jax, jax.numpy as jnp
        import numpy as np
        B, S, D, E, K = (4, 256, 128, 8, 2)
        H = 4 * D
        key = jax.random.key(seed)
        ks = jax.random.split(key, 4)
        sc = lambda n: 1.0 / np.sqrt(n)
        return {'x': jax.random.normal(ks[0], (B, S, D), jnp.float32), 'gate_w': jax.random.normal(ks[1], (D, E), jnp.float32) * sc(D), 'gate_b': jnp.zeros((E,), jnp.float32), 'w1': jax.random.normal(ks[2], (E, D, H), jnp.float32) * sc(D), 'b1': jnp.zeros((E, H), jnp.float32), 'w2': jax.random.normal(ks[3], (E, H, D), jnp.float32) * sc(H), 'b2': jnp.zeros((E, D), jnp.float32)}
    _L0_ffn_in = _L0_ffn_setup()
    _d = {'L0_attn_hidden_states': _L0_attn_in['hidden_states'], 'L0_attn_Wq': _L0_attn_in['Wq'], 'L0_attn_Wk': _L0_attn_in['Wk'], 'L0_attn_Wv': _L0_attn_in['Wv'], 'L0_attn_Wo': _L0_attn_in['Wo'], 'L0_ffn_gate_w': _L0_ffn_in['gate_w'], 'L0_ffn_gate_b': _L0_ffn_in['gate_b'], 'L0_ffn_w1': _L0_ffn_in['w1'], 'L0_ffn_b1': _L0_ffn_in['b1'], 'L0_ffn_w2': _L0_ffn_in['w2'], 'L0_ffn_b2': _L0_ffn_in['b2']}
    _x0 = _d['L0_attn_hidden_states']
    _d['L0_attn_hidden_states'] = jax.random.normal(jax.random.fold_in(jax.random.key(seed), 1), (16, 256, 128), dtype=_x0.dtype)
    del _x0
    return _d

def reference(L0_attn_hidden_states, L0_attn_Wq, L0_attn_Wk, L0_attn_Wv, L0_attn_Wo, L0_ffn_gate_w, L0_ffn_gate_b, L0_ffn_w1, L0_ffn_b1, L0_ffn_w2, L0_ffn_b2):

    def _L0_attn_ref(hidden_states, Wq, Wk, Wv, Wo):
        import jax, jax.numpy as jnp
        import numpy as np
        EPS = 1e-05
        NUM_HEADS = 16
        FEATURE_DIM = 16
        CHUNK = 64

        def _phi(x):
            f = x.shape[-1]
            return (x[..., :, None] * x[..., None, :]).reshape(*x.shape[:-1], f * f)
        b, l, d = hidden_states.shape
        h, f = (NUM_HEADS, FEATURE_DIM)
        hd = d // h
        q = (hidden_states @ Wq).reshape(b, l, h, f).transpose(0, 2, 1, 3)
        k = (hidden_states @ Wk).reshape(b, l, h, f).transpose(0, 2, 1, 3)
        v = (hidden_states @ Wv).reshape(b, l, h, hd).transpose(0, 2, 1, 3)
        q = q * f ** (-0.5)
        n = l // CHUNK
        qc = q.reshape(b, h, n, CHUNK, f)
        kc = k.reshape(b, h, n, CHUNK, f)
        vc = v.reshape(b, h, n, CHUNK, hd)
        phi_q = _phi(qc)
        phi_k = _phi(kc)
        mask = jnp.tril(jnp.ones((CHUNK, CHUNK), dtype=q.dtype))

        def step(carry, inp):
            S, z = carry
            pq, pk, qi, ki, vi = inp
            inter_o = jnp.einsum('bhcf,bhfd->bhcd', pq, S)
            inter_z = jnp.einsum('bhcf,bhf->bhc', pq, z)
            A = jnp.einsum('bhcf,bhsf->bhcs', qi, ki) ** 2 * mask
            intra_o = jnp.einsum('bhcs,bhsd->bhcd', A, vi)
            intra_z = A.sum(-1)
            o = (inter_o + intra_o) / (inter_z + intra_z + EPS)[..., None]
            S = S + jnp.einsum('bhcf,bhcd->bhfd', pk, vi)
            z = z + pk.sum(2)
            return ((S, z), o)
        f2 = f * f
        S0 = jnp.zeros((b, h, f2, hd), q.dtype)
        z0 = jnp.zeros((b, h, f2), q.dtype)
        xs = (jnp.moveaxis(phi_q, 2, 0), jnp.moveaxis(phi_k, 2, 0), jnp.moveaxis(qc, 2, 0), jnp.moveaxis(kc, 2, 0), jnp.moveaxis(vc, 2, 0))
        _, o = jax.lax.scan(step, (S0, z0), xs)
        o = jnp.moveaxis(o, 0, 2).reshape(b, h, l, hd)
        o = o.transpose(0, 2, 1, 3).reshape(b, l, h * hd)
        return o @ Wo

    def _L0_ffn_ref(x, gate_w, gate_b, w1, b1, w2, b2):
        import jax, jax.numpy as jnp
        import numpy as np
        B, S, D, E, K = (4, 256, 128, 8, 2)
        H = 4 * D
        Bx, Sx, Dx = x.shape
        n_exp = w1.shape[0]
        logits = jnp.einsum('bsd,de->bse', x, gate_w) + gate_b
        scores = jax.nn.softmax(logits, axis=-1)
        topk_s, topk_i = jax.lax.top_k(scores, K)
        onehot = jax.nn.one_hot(topk_i, n_exp, dtype=scores.dtype)
        dispatch = jnp.einsum('bske,bsk->bse', onehot, topk_s)
        xf = x.reshape(-1, Dx)
        wf = dispatch.reshape(-1, n_exp)
        out = jnp.zeros_like(xf)
        for i in range(n_exp):
            wi = wf[:, i:i + 1]
            h = jax.nn.relu(xf * wi @ w1[i] + b1[i])
            y = h @ w2[i] + b2[i]
            out = jnp.where(wi > 0, y, out)
        return out.reshape(Bx, Sx, Dx)
    x = L0_attn_hidden_states
    x = x + _L0_attn_ref(_layernorm(x, axis=-1), L0_attn_Wq, L0_attn_Wk, L0_attn_Wv, L0_attn_Wo)
    x = x + _L0_ffn_ref(_layernorm(x, axis=-1), L0_ffn_gate_w, L0_ffn_gate_b, L0_ffn_w1, L0_ffn_b1, L0_ffn_w2, L0_ffn_b2)
    return x

_drawn_inputs = setup_inputs


def setup_inputs(seed=0):
    import zlib

    import numpy as np

    out = dict(_drawn_inputs(seed))
    spreads = {'L0_ffn_gate_b': (0.0, 0.1), 'L0_ffn_b1': (0.0, 0.1), 'L0_ffn_b2': (0.0, 0.1)}
    factors = {}
    for name, (base, spread) in spreads.items():
        noise = np.random.default_rng([zlib.crc32(name.encode()), seed]).standard_normal(out[name].shape)
        drawn = base * np.exp(spread * noise) if base else spread * noise
        out[name] = jnp.asarray(drawn.astype(out[name].dtype))
    for name, factor in factors.items():
        out[name] = (out[name] * factor).astype(out[name].dtype)
    return out
```

```python
import numpy as np
import concourse.bass as bass
from concourse import mybir
from contextlib import ExitStack


class Turn:

    def __init__(self, n, lap, slot):
        self.n, self.lap, self.slot = n, lap, slot


def turn(offset, ring, total, lap=None):
    if lap is None:
        return Turn(offset, offset // ring, offset % ring) if 0 <= offset < total else None
    return Turn(lap * ring + offset, lap + offset // ring, offset % ring)


def after(engine, semaphore, count):
    if not (isinstance(count, int) and count <= 0):
        engine.wait_ge(semaphore, count)


def wait_apart(engine, semaphore, count, met):
    if not isinstance(count, int):
        count = engine.to_reg(count)
    engine.wait_ge(*met)
    engine.wait_ge(semaphore, count)


def attention_moe_kernel(nc, x, Wq, Wk, Wv, Wo, gate_w, gate_b, w1, b1, w2, b2, out):
    fp32 = mybir.dt.float32
    bf16 = mybir.dt.bfloat16
    i32 = mybir.dt.int32
    ALU = mybir.AluOpType
    ACT = mybir.ActivationFunctionType
    AX = mybir.AxisListType

    NB, L, D = x.shape
    P = 128
    NTK = L // P
    H, F, HD = 16, 16, 8
    E, _, FF = w1.shape
    FC = FF // P
    TOK = NB * L
    LN_EPS = 1e-5
    ATT_EPS = 1e-5
    TINY = 1e-30
    Q_SCALE = float(F) ** -0.5

    HG = P // F
    NG = H // HG
    PARTS = 3
    K_SLOTS = (0, 0, 0, 1, 1, 2)
    Q_SLOTS = (0, 1, 2, 0, 1, 0)
    SLOTS = len(K_SLOTS)
    KS = SLOTS * F
    GROUPS = 4
    GH = H // GROUPS
    STRIP = 32
    SUB = 16

    REGION = TOK + P
    ROWW = 2 * D + 4
    IDCOL = 2 * D
    NOWHERE = TOK
    TILES = TOK // P + E - 1
    RING = 4

    region = nc.dram_tensor("expert_rows", (E * REGION + P, ROWW), fp32, kind="Internal").ap()
    scratch = nc.dram_tensor("qk_parts", (2, 2, PARTS, H, F, L), bf16, kind="Internal").ap()

    ctx = ExitStack()
    with ctx:
        def sb(name, shape, dt=fp32):
            return ctx.enter_context(nc.sbuf_tensor(name, shape, dt))

        def sem(name):
            return ctx.enter_context(nc.semaphore(name))

        wq_sb = sb("wq_sb", [P, H * F])
        wk_sb = sb("wk_sb", [P, H * F])
        wv_sb = sb("wv_sb", [P, H * HD])
        wo_sb = sb("wo_sb", [P, D])
        gw_sb = sb("gw_sb", [P, E])
        gb_sb = sb("gb_sb", [P, E])
        w1_sb = sb("w1_sb", [P, E * FF])
        w2_sb = sb("w2_sb", [P, E * FC * D])
        b1_sb = sb("b1_sb", [P, E * FF])
        b2_sb = sb("b2_sb", [P, E * D])
        ident = sb("ident", [P, P])
        before = sb("before", [P, P], bf16)
        ones = sb("ones", [P, P], bf16)
        minus_half = sb("minus_half", [P, NTK])
        number1_i = sb("number1_i", [P, E], i32)
        number1 = sb("number1", [P, E])
        ties = sb("ties", [P, E, E])
        token_i = sb("token_i", [P, NTK], i32)
        token = sb("token", [P, NTK])
        base = sb("base", [P, E])
        pad_rows = sb("pad_rows", [P, ROWW])
        tile_i = sb("tile_i", [1, TILES], i32)
        tile_no = sb("tile_no", [1, TILES])

        x_ln = [sb(f"x_ln{i}", [P, NTK, D]) for i in range(2)]
        x_res = [sb(f"x_res{i}", [P, NTK, D]) for i in range(2)]
        stats1 = sb("stats1", [P, NTK, 6])
        mv1 = sb("mv1", [P, NTK, 2])
        ve1 = sb("ve1", [P, NTK])
        rstd1 = sb("rstd1", [P, NTK])
        xn = sb("xn", [P, NTK, D])
        xnT = [sb(f"xnT{i}", [P, L]) for i in range(2)]
        parts = [[sb(f"parts{o}{i}", [P, PARTS, NG * L], bf16) for i in range(2)] for o in range(2)]
        rest = [sb(f"rest{o}", [P, NG * L]) for o in range(2)]
        stack = [[sb(f"stack{o}{i}", [KS, H, L], bf16) for i in range(2)] for o in range(2)]
        v_ext = [sb(f"v_ext{i}", [P, NTK, 2, H // 2, STRIP]) for i in range(2)]
        scores = [sb(f"scores{g}", [P, 3, GH, P]) for g in range(GROUPS)]
        u_sb = [sb(f"u_sb{g}", [P, L]) for g in range(NG)]
        den = sb("den", [P, NG * NTK, HG])
        rden = sb("rden", [P, NG * NTK, HG])
        o_sb = sb("o_sb", [P, NTK, NG, HG * HD])
        oT = sb("oT", [P, L])

        row = [sb(f"row{i}", [P, NTK, ROWW]) for i in range(2)]
        stats2 = sb("stats2", [P, NTK, 6])
        mv2 = sb("mv2", [P, NTK, 2])
        ve2 = sb("ve2", [P, NTK])
        rstd2 = sb("rstd2", [P, NTK])
        x2n = [sb(f"x2n{i}", [P, NTK, D]) for i in range(2)]
        x2nT = sb("x2nT", [P, L])
        logit = sb("logit", [P, NTK, E])
        top = sb("top", [P, NTK])
        shifted = sb("shifted", [P, NTK, E])
        expo = sb("expo", [P, NTK, E])
        esum = sb("esum", [P, NTK])
        rsum = sb("rsum", [P, NTK])
        score = sb("score", [P, NTK, E])
        gap = sb("gap", [P, NTK, E, E])
        ahead = sb("ahead", [P, NTK, E, E])
        rank = sb("rank", [P, NTK, E])
        key0 = sb("key0", [P, NTK, E])
        key = sb("key", [P, NTK, E])
        chosen = sb("chosen", [P, NTK])
        onehot = sb("onehot", [P, NTK, E], bf16)
        picked = sb("picked", [P, NTK, E])
        weight = sb("weight", [P, NTK])
        place = sb("place", [P, NTK, E])
        placed = sb("placed", [P, NTK, E])
        nth = sb("nth", [P, NTK])
        slot_i = [sb(f"slot_i{i}", [P, NTK], i32) for i in range(2)]

        count = sb("count", [1, E])
        count_i = sb("count_i", [1, E], i32)
        ntile_f = sb("ntile_f", [1, E])
        ntile_i = sb("ntile_i", [1, E], i32)
        cum = [sb(f"cum{i}", [1, E]) for i in range(4)]
        passed = sb("passed", [1, TILES, E])
        tile_e = sb("tile_e", [1, TILES])
        passed_c = sb("passed_c", [1, TILES, E])
        first = sb("first", [1, TILES])
        local = sb("local", [1, TILES])
        e_row = sb("e_row", [1, TILES])
        t_row = sb("t_row", [1, TILES])
        row_i = sb("row_i", [1, TILES], i32)
        expert_i = sb("expert_i", [1, TILES], i32)

        xr = [sb(f"xr{i}", [P, ROWW]) for i in range(RING)]
        xwT = [sb(f"xwT{i}", [P, P]) for i in range(2)]
        hb = [sb(f"hb{i}", [P, FF]) for i in range(2)]
        hT = [sb(f"hT{i}", [P, FF]) for i in range(2)]
        x2b = [sb(f"x2b{i}", [P, D]) for i in range(2)]
        y_sb = [sb(f"y_sb{i}", [P, D]) for i in range(RING)]

        bank = [ctx.enter_context(nc.psum_tensor(f"bank{i}", [P, 512], fp32)) for i in range(8)]
        score_bank = bank[0:3]
        av_bank = bank[3:5]
        p5, p6, p7 = bank[5], bank[6], bank[7]
        up_bank = bank[0:2]
        xw_bank = bank[2]
        hT_bank = bank[3:5]
        down_bank = bank[5:7]

        attn_w = sem("attn_w")
        moe_w = sem("moe_w")
        pads_in = sem("pads_in")
        pool_const = sem("pool_const")
        pool_step = sem("pool_step")
        dve_const = sem("dve_const")
        x_ln_in = [sem(f"x_ln_in{i}") for i in range(2)]
        x_res_in = [sem(f"x_res_in{i}") for i in range(2)]
        ln1_step = sem("ln1_step")
        ln1_stats = sem("ln1_stats")
        ln1_var = sem("ln1_var")
        ln1_rstd = sem("ln1_rstd")
        xn_ready = sem("xn_ready")
        tn_done = sem("tn_done")
        xnT_ready = sem("xnT_ready")
        proj_done = [sem("q_done"), sem("k_done")]
        high_ready = [sem("q_high"), sem("k_high")]
        rest_ready = [sem("q_rest"), sem("k_rest")]
        mid_ready = [sem("q_mid"), sem("k_mid")]
        low_ready = [sem("q_low"), sem("k_low")]
        parts_out = [sem(f"parts_out{i}") for i in range(2)]
        stack_in = [sem(f"stack_in{i}") for i in range(2)]
        v_done = sem("v_done")
        v_ready = sem("v_ready")
        scored = sem("scored")
        squared = sem("squared")
        masked = sem("masked")
        av_done = sem("av_done")
        u_ready = sem("u_ready")
        tu_done = sem("tu_done")
        den_step = sem("den_step")
        o_ready = sem("o_ready")
        to_done = sem("to_done")
        oT_ready = sem("oT_ready")
        wo_done = sem("wo_done")
        x2_ready = sem("x2_ready")
        ln2_step = sem("ln2_step")
        ln2_stats = sem("ln2_stats")
        ln2_var = sem("ln2_var")
        ln2_rstd = sem("ln2_rstd")
        x2n_ready = sem("x2n_ready")
        tx_done = sem("tx_done")
        x2nT_ready = sem("x2nT_ready")
        gate_done = sem("gate_done")
        logit_ready = sem("logit_ready")
        gap_ready = sem("gap_ready")
        shifted_ready = sem("shifted_ready")
        expo_ready = sem("expo_ready")
        route_step = sem("route_step")
        onehot_ready = sem("onehot_ready")
        prefix_done = sem("prefix_done")
        prefix_read = sem("prefix_read")
        row_ready = sem("row_ready")
        rows_out = [sem(f"rows_out{i}") for i in range(2)]
        table_step = sem("table_step")
        counts_ready = sem("counts_ready")
        table_ready = sem("table_ready")
        xr_in = [sem(f"xr_in{i}") for i in range(RING)]
        xwt_done = sem("xwt_done")
        xwT_ready = sem("xwT_ready")
        up_done = sem("up_done")
        hb_ready = sem("hb_ready")
        ht_done = sem("ht_done")
        hT_ready = sem("hT_ready")
        down_done = sem("down_done")
        x2b_ready = sem("x2b_ready")
        y_ready = sem("y_ready")
        y_out = [sem(f"y_out{i}") for i in range(RING)]

        ROUTE_STEPS = 15
        consts = (pool_const, 2)
        ATTN_WEIGHTS = 6 * 16
        MOE_WEIGHTS = 4 * 16

        PERIODS = NB + 4
        LOOP_FROM, LOOP_LAPS = 4, (NB - 6) // 2

        def periods(engine, period):
            def item_at(p, lap=None):
                return lambda lag, total=NB: turn(p - lag, 2, total, lap)

            for p in range(LOOP_FROM):
                period(item_at(p))
            with engine.Fori(0, LOOP_LAPS) as lap:
                for p in range(LOOP_FROM, LOOP_FROM + 2):
                    period(item_at(p, lap))
            for p in range(LOOP_FROM + 2 * LOOP_LAPS, PERIODS):
                period(item_at(p))

        def upto(count):
            return min(count, NB) if isinstance(count, int) else count

        def steps(engine, step):
            def item_at(s, lap=None):
                return lambda lag: turn(s - lag, RING, TILES, lap)

            laps = (TILES - 3 - RING) // RING
            for s in range(RING):
                step(item_at(s))
            with engine.Fori(0, laps) as lap:
                for s in range(RING, 2 * RING):
                    step(item_at(s, lap))
            for s in range(RING + RING * laps, TILES + 2):
                step(item_at(s))

        block = ctx.enter_context(nc.Block())

        @block.sync
        def _(sp):
            def load_stacks(b):
                after(sp, parts_out[b.slot], 32 * (b.lap + 1))
                after(sp, scored, 12 * (b.n - 1))
                for o, slots in ((0, Q_SLOTS), (1, K_SLOTS)):
                    for s, part in enumerate(slots):
                        sp.dma_start(stack[o][b.slot][F * s:F * (s + 1), :, :],
                                     scratch[b.slot, o, part].rearrange("h f t -> f h t")
                                     ).then_inc(stack_in[b.slot], 16)

            def load_x(b):
                after(sp, xn_ready, b.n - 1)
                sp.dma_start(x_ln[b.slot][:, :, :], x_tiles(b)).then_inc(x_ln_in[b.slot], 16)

            def load_residual(b):
                after(sp, x2_ready, b.n - 1)
                sp.dma_start(x_res[b.slot][:, :, :], x_tiles(b)).then_inc(x_res_in[b.slot], 16)

            def x_tiles(b):
                return x[bass.ds(b.n, 1)].rearrange("a (j p) d -> p (a j) d", p=P)

            def store_parts(b, o):
                wait_apart(sp, low_ready[o], b.n + 1, consts)
                if o == 0:
                    after(sp, stack_in[b.slot], 16 * 2 * SLOTS * b.lap)
                sp.dma_start(scratch[b.slot, o].rearrange("a (g h) f t -> (h f) a g t", g=NG),
                             parts[o][b.slot][:, :, :].rearrange("p a (g t) -> p a g t", g=NG)
                             ).then_inc(parts_out[b.slot], 16)

            for dst, src in ((wq_sb, Wq), (wk_sb, Wk), (wv_sb, Wv), (wo_sb, Wo), (gw_sb, gate_w)):
                if dst is wq_sb:
                    load_x(turn(0, 2, NB))
                sp.dma_start(dst[:, :], src).then_inc(attn_w, 16)
            sp.dma_start(gb_sb[:, :], gate_b.partition_broadcast(P)).then_inc(attn_w, 16)
            load_x(turn(1, 2, NB))

            def period(at):
                if (b := at(1)):
                    load_stacks(b)
                if (b := at(-2)):
                    load_x(b)
                if (b := at(2)):
                    load_residual(b)
                if (b := at(0)):
                    store_parts(b, 0)
                    store_parts(b, 1)

            periods(sp, period)

            sp.wait_ge(counts_ready, 1)
            sp.wait_ge(pool_const, 1)
            for e in range(E):
                n = sp.value_load(count_i[0:1, e:e + 1], min_val=0, max_val=TOK)
                sp.dma_start(region[bass.ds(n + e * REGION, P), :], pad_rows[:, :]).then_inc(pads_in, 16)
            for i in range(2):
                sp.wait_ge(rows_out[i], 16 * NTK * (NB // 2))
            sp.wait_ge(pads_in, 16 * (E + 1))
            sp.wait_ge(table_ready, 1)

            def load_tile(t):
                after(sp, y_out[t.slot], 16 * t.lap)
                at_row = sp.value_load(row_i[0:1, bass.ds(t.n, 1)], min_val=0, max_val=E * REGION)
                sp.dma_start(xr[t.slot][:, :], region[bass.ds(at_row, P), :]).then_inc(xr_in[t.slot], 16)

            with sp.Fori(0, TILES // RING) as lap:
                for s in range(RING):
                    load_tile(turn(s, RING, TILES, lap))
            for s in range(TILES // RING * RING, TILES):
                load_tile(turn(s, RING, TILES))
            for i in range(RING):
                sp.wait_ge(y_out[i], 16 * ((TILES - 1 - i) // RING + 1))

        @block.scalar
        def _(act):
            act.dma_start(w1_sb[:, :].rearrange("p (e n) -> p e n", e=E),
                          w1.rearrange("e d n -> d e n")).then_inc(moe_w, 16)
            act.dma_start(w2_sb[:, :].rearrange("p (e c n) -> p e c n", e=E, c=FC),
                          w2.rearrange("e (c f) n -> f e c n", c=FC)).then_inc(moe_w, 16)
            act.dma_start(b1_sb[:, :], b1.rearrange("e n -> (e n)").partition_broadcast(P)).then_inc(moe_w, 16)
            act.dma_start(b2_sb[:, :], b2.rearrange("e n -> (e n)").partition_broadcast(P)).then_inc(moe_w, 16)
            act.wait_ge(pool_const, 1)
            act.dma_start(region[E * REGION:E * REGION + P, :], pad_rows[:, :]).then_inc(pads_in, 16)

            def square(b, g):
                for k in range(3):
                    act.wait_ge(scored, 12 * b.n + 3 * g + k + 1)
                    if k == 0:
                        after(act, av_done, GROUPS * (b.n - 1) + g + 1)
                    nc.scalar.activation(scores[g][:, k, :, :].rearrange("p h t -> p (h t)"),
                                         score_bank[k][:, :], ACT.Square, scale=Q_SCALE).then_inc(squared, 1)

            def exponent(b):
                act.wait_ge(shifted_ready, b.n + 1)
                after(act, onehot_ready, b.n)
                nc.scalar.activation(expo[:, :, :], shifted[:, :, :], ACT.Exp).then_inc(expo_ready, 1)

            def copy_xnT(b):
                act.wait_ge(tn_done, b.n + 1)
                after(act, v_done, b.n - 1)
                nc.scalar.copy(xnT[b.slot][:, :], p6[:, 0:L]).then_inc(xnT_ready, 1)

            def high(b, o):
                act.wait_ge(proj_done[o], b.n + 1)
                after(act, parts_out[b.slot], 32 * b.lap)
                nc.scalar.copy(parts[o][b.slot][:, 0, :], (p6, p5)[o][:, :]).then_inc(high_ready[o], 1)

            def copy_u(b, g):
                act.wait_ge(av_done, GROUPS * b.n + 2 * g + 2)
                after(act, tu_done, b.n)
                nc.scalar.copy(u_sb[g][:, :], av_bank[g][:, 0:L]).then_inc(u_ready, 1)

            def copy_oT(b):
                act.wait_ge(to_done, b.n + 1)
                after(act, wo_done, b.n)
                nc.scalar.copy(oT[:, :], p7[:, 0:L]).then_inc(oT_ready, 1)

            def copy_x2nT(b):
                act.wait_ge(tx_done, b.n + 1)
                after(act, gate_done, b.n)
                nc.scalar.copy(x2nT[:, :], p6[:, 0:L]).then_inc(x2nT_ready, 1)

            def period(at):
                new, core, tail, route = at(0), at(2), at(3), at(4)
                if core:
                    square(core, 0)
                if route:
                    exponent(route)
                if new:
                    copy_xnT(new)
                if core:
                    square(core, 1)
                if tail:
                    copy_oT(tail)
                if new:
                    high(new, 0)
                if core:
                    square(core, 2)
                    copy_u(core, 0)
                if new:
                    high(new, 1)
                if core:
                    square(core, 3)
                if tail:
                    copy_x2nT(tail)
                if core:
                    copy_u(core, 1)

            periods(act, period)

            def step(at):
                if (t := at(1)):
                    act.wait_ge(ht_done, t.n + 1)
                    after(act, down_done, t.n - 1)
                    nc.scalar.activation(hT[t.slot % 2][:, :], hT_bank[t.slot % 2][:, :],
                                         ACT.Relu).then_inc(hT_ready, 1)
                if (t := at(-1)):
                    copy_xwT(t)

            def copy_xwT(t):
                act.wait_ge(xwt_done, t.n + 1)
                after(act, up_done, t.n - 1)
                nc.scalar.copy(xwT[t.slot % 2][:, :], xw_bank[:, 0:P]).then_inc(xwT_ready, 1)

            copy_xwT(turn(0, RING, TILES))
            steps(act, step)

        @block.gpsimd
        def _(pool):
            nc.gpsimd.memset(pad_rows[:, :], 0.0).then_inc(pool_step, 1)
            nc.gpsimd.memset(ident[:, :], 0.0)
            nc.gpsimd.memset(before[:, :], 1.0)
            nc.gpsimd.memset(ones[:, :], 1.0)
            nc.gpsimd.memset(minus_half[:, :], -0.5)
            nc.gpsimd.memset(ties[:, :, :], -TINY)
            nc.gpsimd.memset(base[:, :], -float(REGION)).then_inc(pool_step, 1)
            pool.wait_ge(pool_step, 2)
            nc.gpsimd.memset(pad_rows[:, IDCOL:IDCOL + 1].bitcast(i32), NOWHERE).then_inc(pool_const, 1)
            nc.gpsimd.affine_select(out=ident[:, :], in_=ident[:, :], compare_op=ALU.not_equal, fill=1.0,
                                    base=0, pattern=[[-1, P]], channel_multiplier=1)
            nc.gpsimd.affine_select(out=before[:, :], in_=before[:, :], compare_op=ALU.is_gt, fill=0.0,
                                    base=0, pattern=[[1, P]], channel_multiplier=-1)
            nc.gpsimd.affine_select(out=ties[:, :, :], in_=ties[:, :, :], compare_op=ALU.is_gt, fill=TINY,
                                    base=0, pattern=[[1, E], [-1, E]], channel_multiplier=0)
            nc.gpsimd.iota(number1_i[:, :], pattern=[[1, E]], base=1, channel_multiplier=0)
            nc.gpsimd.iota(tile_i[:, :], pattern=[[1, TILES]], base=0, channel_multiplier=0)
            nc.gpsimd.iota(token_i[:, :], pattern=[[P, NTK]], base=0, channel_multiplier=1).then_inc(pool_step, 1)
            pool.wait_ge(pool_step, 3)
            nc.gpsimd.tensor_copy(number1[:, :], number1_i[:, :])
            nc.gpsimd.tensor_copy(tile_no[:, :], tile_i[:, :])
            nc.gpsimd.tensor_copy(token[:, :], token_i[:, :]).then_inc(pool_const, 1)

            def mask(b, g):
                for k, of in ((0, 1), (2, 3)):
                    wait_apart(pool, squared, 12 * b.n + 3 * g + of, consts)
                    nc.gpsimd.affine_select(out=scores[g][:, k, :, :], in_=scores[g][:, k, :, :],
                                            compare_op=ALU.is_ge, fill=0.0, base=0,
                                            pattern=[[0, GH], [1, P]], channel_multiplier=-1).then_inc(masked, 1)

            def reciprocal_root(b, mv, ve, rstd, stats, var, done):
                wait_apart(pool, stats, b.n + 1, consts)
                nc.gpsimd.tensor_scalar_add(ve[:, :], mv[:, :, 1], LN_EPS).then_inc(var, 1)
                pool.wait_ge(var, b.n + 1)
                nc.gpsimd.tensor_tensor(rstd[:, :], ve[:, :], minus_half[:, :], ALU.pow).then_inc(done, 1)

            def low(b, o):
                pool.wait_ge(mid_ready[o], b.n + 1)
                nc.gpsimd.tensor_tensor(parts[o][b.slot][:, 2, :], rest[o][:, :], parts[o][b.slot][:, 1, :],
                                        ALU.subtract).then_inc(low_ready[o], 1)

            def compare(b):
                pool.wait_ge(logit_ready, b.n + 1)
                after(pool, onehot_ready, b.n)
                for j in range(NTK):
                    last = nc.gpsimd.tensor_tensor(gap[:, j, :, :], logit[:, j, :].unsqueeze(1).broadcast_to([P, E, E]),
                                                   logit[:, j, :].unsqueeze(2).broadcast_to([P, E, E]), ALU.subtract)
                last.then_inc(gap_ready, 1)

            def scatter(b):
                wait_apart(pool, row_ready, b.n + 1, consts)
                for j in range(NTK):
                    nc.gpsimd.indirect_dma_start(
                        out=region, out_offset=bass.IndirectOffsetOnAxis(ap=slot_i[b.slot][:, j:j + 1], axis=0),
                        in_=row[b.slot][:, j, :], in_offset=None).then_inc(rows_out[b.slot], 16)

            def norm1(b):
                reciprocal_root(b, mv1, ve1, rstd1, ln1_stats, ln1_var, ln1_rstd)

            norm1(turn(0, 2, NB))

            def period(at):
                new, core, tail, route, ahead_ = at(0), at(2), at(3), at(4), at(-1)
                if core:
                    mask(core, 0)
                if route:
                    compare(route)
                if core:
                    mask(core, 1)
                if new:
                    low(new, 0)
                if core:
                    mask(core, 2)
                if tail:
                    reciprocal_root(tail, mv2, ve2, rstd2, ln2_stats, ln2_var, ln2_rstd)
                if new:
                    low(new, 1)
                if core:
                    mask(core, 3)
                if ahead_:
                    norm1(ahead_)
                if route:
                    scatter(route)

            periods(pool, period)
            pool.wait_ge(moe_w, MOE_WEIGHTS)
            pool.wait_ge(table_ready, 1)

            def add_bias(t):
                e = pool.value_load(expert_i[0:1, bass.ds(t.n, 1)], min_val=0, max_val=E - 1)
                pool.wait_ge(xr_in[t.slot], 16 * (t.lap + 1))
                after(pool, y_ready, t.n - 1)
                nc.gpsimd.tensor_tensor(x2b[t.slot % 2][:, :], xr[t.slot][:, D:2 * D],
                                        b2_sb[:, bass.ds(e * D, D)], ALU.add).then_inc(x2b_ready, 1)

            def scatter_out(t):
                wait_apart(pool, y_ready, t.n + 1, consts)
                nc.gpsimd.indirect_dma_start(
                    out=out.rearrange("b l d -> (b l) d"),
                    out_offset=bass.IndirectOffsetOnAxis(ap=xr[t.slot][:, IDCOL:IDCOL + 1].bitcast(i32), axis=0),
                    in_=y_sb[t.slot][:, :], in_offset=None,
                    bounds_check=TOK - 1, oob_is_err=False).then_inc(y_out[t.slot], 16)

            def step(at):
                if (t := at(0)):
                    add_bias(t)
                if (t := at(2)):
                    scatter_out(t)

            steps(pool, step)

        @block.vector
        def _(dve):
            for i in range(2):
                nc.vector.memset(v_ext[i][:, :, :, :, :], 0.0)
                nc.vector.memset(row[i][:, :, :], 0.0).then_inc(dve_const, 1)
            dve.wait_ge(dve_const, 2)
            for i in range(2):
                for r in range(2):
                    nc.vector.memset(v_ext[i][:, :, r, :, SUB * r + HD:SUB * r + HD + 1], 1.0)
            dve.wait_ge(pool_const, 2)

            def norm_stats(b, src, stats, mv, step, done):
                for j in range(NTK):
                    ins = nc.vector.bn_stats(stats[:, j, :], src[:, j, :])
                ins.then_inc(step, 1)
                wait_apart(dve, step, b.n + 1, consts)
                for j in range(NTK):
                    ins = nc.vector.bn_aggr(mv[:, j, :], stats[:, j, :])
                ins.then_inc(done, 1)

            def norm1_stats(b):
                dve.wait_ge(x_ln_in[b.slot], 16 * (b.lap + 1))
                norm_stats(b, x_ln[b.slot], stats1, mv1, ln1_step, ln1_stats)

            def norm1_apply(b):
                dve.wait_ge(ln1_rstd, b.n + 1)
                after(dve, tn_done, b.n)
                for j in range(NTK):
                    ins = nc.vector.tensor_scalar(xn[:, j, :], x_ln[b.slot][:, j, :], mv1[:, j, 0:1],
                                                  rstd1[:, j:j + 1], ALU.subtract, ALU.mult)
                ins.then_inc(xn_ready, 1)

            def split(b, o):
                dve.wait_ge(high_ready[o], b.n + 1)
                after(dve, low_ready[o], b.n)
                nc.vector.tensor_tensor(rest[o][:, :], (p6, p5)[o][:, :], parts[o][b.slot][:, 0, :],
                                        ALU.subtract).then_inc(rest_ready[o], 1)
                dve.wait_ge(rest_ready[o], b.n + 1)
                nc.vector.tensor_copy(parts[o][b.slot][:, 1, :], rest[o][:, :]).then_inc(mid_ready[o], 1)

            def place_v(b):
                dve.wait_ge(v_done, b.n + 1)
                after(dve, av_done, GROUPS * (b.n - 1))
                for r in range(2):
                    ins = nc.vector.tensor_copy(
                        v_ext[b.slot][:, :, r, :, SUB * r:SUB * r + HD],
                        p5[:, 0:NTK * H * HD].rearrange("p (j x r d) -> p j x r d", j=NTK, r=2, d=HD)[:, :, :, r, :])
                ins.then_inc(v_ready, 1)

            def divide(b):
                dve.wait_ge(tu_done, b.n + 1)
                heads = p5[:, :].rearrange("p (j h w) -> p j h w", h=HG, w=SUB)
                nc.vector.tensor_scalar_add(den[:, :, :], heads[:, :, :, HD], ATT_EPS).then_inc(den_step, 1)
                dve.wait_ge(den_step, 2 * b.n + 1)
                nc.vector.reciprocal(rden[:, :, :], den[:, :, :]).then_inc(den_step, 1)
                dve.wait_ge(den_step, 2 * b.n + 2)
                after(dve, to_done, b.n)
                nc.vector.tensor_tensor(o_sb[:, :, :, :].rearrange("p j g (h d) -> p (j g) h d", d=HD),
                                        heads[:, :, :, 0:HD],
                                        rden[:, :, :].unsqueeze(3).broadcast_to([P, NG * NTK, HG, HD]),
                                        ALU.mult).then_inc(o_ready, 1)

            def residual(b):
                dve.wait_ge(wo_done, b.n + 1)
                dve.wait_ge(x_res_in[b.slot], 16 * (b.lap + 1))
                after(dve, rows_out[b.slot], 16 * NTK * b.lap)
                nc.vector.tensor_tensor(row[b.slot][:, :, D:2 * D],
                                        p7[:, 0:NTK * D].rearrange("p (j d) -> p j d", j=NTK),
                                        x_res[b.slot][:, :, :], ALU.add).then_inc(x2_ready, 1)
                dve.wait_ge(x2_ready, b.n + 1)
                norm_stats(b, row[b.slot][:, :, D:2 * D], stats2, mv2, ln2_step, ln2_stats)

            def norm2_apply(b):
                dve.wait_ge(ln2_rstd, b.n + 1)
                after(dve, tx_done, b.n - 1)
                for j in range(NTK):
                    ins = nc.vector.tensor_scalar(x2n[b.slot][:, j, :], row[b.slot][:, j, D:2 * D],
                                                  mv2[:, j, 0:1], rstd2[:, j:j + 1], ALU.subtract, ALU.mult)
                ins.then_inc(x2n_ready, 1)

            def wide(ap):
                return ap.unsqueeze(2).broadcast_to([P, NTK, E])

            def shared(ap):
                return ap.unsqueeze(1).broadcast_to([P, NTK, E])

            def route_logits(b):
                dve.wait_ge(gate_done, b.n + 1)
                nc.vector.tensor_tensor(logit[:, :, :], p7[:, 0:NTK * E].rearrange("p (j e) -> p j e", j=NTK),
                                        shared(gb_sb[:, :]), ALU.add).then_inc(logit_ready, 1)
                dve.wait_ge(logit_ready, b.n + 1)
                nc.vector.reduce_max(top[:, :], logit[:, :, :], AX.X).then_inc(route_step, 1)
                dve.wait_ge(route_step, ROUTE_STEPS * b.n + 1)
                nc.vector.tensor_tensor(shifted[:, :, :], logit[:, :, :], wide(top[:, :]),
                                        ALU.subtract).then_inc(shifted_ready, 1)

            def route_choice(b):
                def stepped(k, ins):
                    ins.then_inc(route_step, 1)
                    dve.wait_ge(route_step, ROUTE_STEPS * b.n + k)

                dve.wait_ge(expo_ready, b.n + 1)
                stepped(2, nc.vector.reduce_sum(esum[:, :], expo[:, :, :], AX.X))
                stepped(3, nc.vector.reciprocal(rsum[:, :], esum[:, :]))
                stepped(4, nc.vector.tensor_tensor(score[:, :, :], expo[:, :, :], wide(rsum[:, :]), ALU.mult))
                stepped(5, nc.vector.scalar_tensor_tensor(out=key0[:, :, :], in0=score[:, :, :], scalar=0.0,
                                                          in1=shared(number1[:, :]), op0=ALU.is_gt, op1=ALU.mult))
                dve.wait_ge(gap_ready, b.n + 1)
                stepped(6, nc.vector.tensor_tensor(ahead[:, :, :, :], gap[:, :, :, :],
                                                   ties[:, :, :].unsqueeze(1).broadcast_to([P, NTK, E, E]),
                                                   ALU.is_ge))
                stepped(7, nc.vector.reduce_sum(rank[:, :, :], ahead[:, :, :, :], AX.X))
                stepped(8, nc.vector.scalar_tensor_tensor(out=key[:, :, :], in0=rank[:, :, :], scalar=1.5,
                                                          in1=key0[:, :, :], op0=ALU.is_lt, op1=ALU.mult))
                stepped(9, nc.vector.reduce_max(chosen[:, :], key[:, :, :], AX.X))
                after(dve, prefix_done, b.n)
                nc.vector.tensor_tensor(onehot[:, :, :], key[:, :, :], wide(chosen[:, :]),
                                        ALU.is_equal).then_inc(onehot_ready, 1)
                dve.wait_ge(onehot_ready, b.n + 1)
                stepped(10, nc.vector.tensor_tensor(picked[:, :, :], onehot[:, :, :], score[:, :, :], ALU.mult))
                stepped(11, nc.vector.reduce_sum(weight[:, :], picked[:, :, :], AX.X))
                for j in range(NTK):
                    nc.vector.tensor_scalar(row[b.slot][:, j, 0:D], x2n[b.slot][:, j, :], weight[:, j:j + 1], None,
                                            ALU.mult)
                nc.vector.tensor_copy(row[b.slot][:, :, IDCOL].bitcast(i32), token[:, :])
                stepped(12, nc.vector.tensor_scalar_add(token[:, :], token[:, :], float(L)))

            def route_place(b):
                dve.wait_ge(prefix_done, b.n + 1)
                nc.vector.tensor_tensor(place[:, :, :], p7[:, 0:NTK * E].rearrange("p (j e) -> p j e", j=NTK),
                                        shared(base[:, :]), ALU.add).then_inc(route_step, 1)
                dve.wait_ge(route_step, ROUTE_STEPS * b.n + 13)
                nc.vector.tensor_tensor(base[:, :], base[:, :], p7[:, NTK * E:(NTK + 1) * E],
                                        ALU.add).then_inc(prefix_read, 1)
                nc.vector.tensor_tensor(placed[:, :, :], onehot[:, :, :], place[:, :, :],
                                        ALU.mult).then_inc(route_step, 1)
                dve.wait_ge(route_step, ROUTE_STEPS * b.n + 14)
                nc.vector.reduce_sum(nth[:, :], placed[:, :, :], AX.X).then_inc(route_step, 1)
                dve.wait_ge(route_step, ROUTE_STEPS * b.n + 15)
                nc.vector.scalar_tensor_tensor(out=slot_i[b.slot][:, :], in0=chosen[:, :], scalar=float(REGION),
                                               in1=nth[:, :], op0=ALU.mult, op1=ALU.add).then_inc(row_ready, 1)

            norm1_stats(turn(0, 2, NB))
            norm1_apply(turn(0, 2, NB))
            dve.wait_ge(attn_w, ATTN_WEIGHTS)

            def period(at):
                new, vb, tail, route, ahead_ = at(0), at(1), at(3), at(4), at(-1)
                if route:
                    route_logits(route)
                if tail:
                    divide(tail)
                if route:
                    route_choice(route)
                if new:
                    split(new, 0)
                if tail:
                    residual(tail)
                if new:
                    split(new, 1)
                if tail:
                    norm2_apply(tail)
                if vb:
                    place_v(vb)
                if ahead_:
                    norm1_stats(ahead_)
                if route:
                    route_place(route)
                if ahead_:
                    norm1_apply(ahead_)

            periods(dve, period)

            ts = [0]

            def stepped(ins):
                ts[0] += 1
                ins.then_inc(table_step, 1)
                dve.wait_ge(table_step, ts[0])

            dve.wait_ge(prefix_read, NB)
            stepped(nc.vector.tensor_scalar_add(count[:, :], base[0:1, :], float(REGION)))
            nc.vector.tensor_copy(count_i[:, :], count[:, :]).then_inc(counts_ready, 1)
            stepped(nc.vector.tensor_scalar(ntile_f[:, :], count[:, :], 1.0 / P,
                                            (P - 1) / P - 0.5 + 0.5 / P, ALU.mult, ALU.add))
            stepped(nc.vector.tensor_copy(ntile_i[:, :], ntile_f[:, :]))
            stepped(nc.vector.tensor_copy(cum[0][:, :], ntile_i[:, :]))
            for k in range(3):
                d = 1 << k
                nc.vector.tensor_copy(cum[k + 1][:, 0:d], cum[k][:, 0:d])
                stepped(nc.vector.tensor_tensor(cum[k + 1][:, d:E], cum[k][:, d:E], cum[k][:, 0:E - d], ALU.add))
            per_tile = cum[3][:, :].unsqueeze(1).broadcast_to([1, TILES, E])
            stepped(nc.vector.tensor_tensor(passed[:, :, :],
                                            tile_no[:, :].unsqueeze(2).broadcast_to([1, TILES, E]),
                                            per_tile, ALU.is_ge))
            nc.vector.reduce_sum(tile_e[:, :], passed[:, :, :], AX.X)
            stepped(nc.vector.tensor_tensor(passed_c[:, :, :], passed[:, :, :], per_tile, ALU.mult))
            stepped(nc.vector.reduce_max(first[:, :], passed_c[:, :, :], AX.X))
            nc.vector.tensor_tensor(local[:, :], tile_no[:, :], first[:, :], ALU.subtract)
            stepped(nc.vector.tensor_scalar(e_row[:, :], tile_e[:, :], float(REGION), None, ALU.mult))
            stepped(nc.vector.scalar_tensor_tensor(out=t_row[:, :], in0=local[:, :], scalar=float(P),
                                                   in1=e_row[:, :], op0=ALU.mult, op1=ALU.add))
            nc.vector.tensor_scalar(row_i[:, :], t_row[:, :], float(E * REGION), None, ALU.min)
            nc.vector.tensor_scalar(expert_i[:, :], tile_e[:, :], float(E - 1), None,
                                    ALU.min).then_inc(table_ready, 1)
            dve.wait_ge(table_ready, 1)
            dve.wait_ge(moe_w, MOE_WEIGHTS)

            def step(at):
                if (t := at(0)):
                    dve.wait_ge(up_done, t.n + 1)
                    after(dve, ht_done, t.n - 1)
                    e = dve.value_load(expert_i[0:1, bass.ds(t.n, 1)], min_val=0, max_val=E - 1)
                    nc.vector.tensor_tensor(hb[t.slot % 2][:, :], up_bank[t.slot % 2][:, :],
                                            b1_sb[:, bass.ds(e * FF, FF)], ALU.add).then_inc(hb_ready, 1)
                if (t := at(2)):
                    dve.wait_ge(down_done, t.n + 1)
                    dve.wait_ge(x2b_ready, t.n + 1)
                    after(dve, y_out[t.slot], 16 * t.lap)
                    nc.vector.tensor_tensor(y_sb[t.slot][:, :], down_bank[t.slot % 2][:, 0:D],
                                            x2b[t.slot % 2][:, :], ALU.add).then_inc(y_ready, 1)

            steps(dve, step)

        @block.tensor
        def _(pe):
            def mm(o, l, r, start=True, stop=True):
                return nc.tensor.matmul(o, lhsT=l, rhs=r, start=start, stop=stop)

            def transpose(o, i):
                return nc.tensor.transpose(o, i, ident[:, :])

            def score(b, g):
                if g == 0:
                    pe.wait_ge(stack_in[b.slot], 16 * 2 * SLOTS * (b.lap + 1))
                qs, ks = stack[0][b.slot], stack[1][b.slot]
                for k, (kt, qt) in enumerate(((0, 0), (0, 1), (1, 1))):
                    after(pe, squared, 12 * b.n + 3 * (g - 1) + k + 1)
                    for c in range(GH):
                        h = HG * (g // 2) + 2 * c + g % 2
                        last = mm(score_bank[k][:, c * P:(c + 1) * P], ks[:, h, kt * P:(kt + 1) * P],
                                  qs[:, h, qt * P:(qt + 1) * P])
                    last.then_inc(scored, 1)

            def weigh(b, g):
                gg, r = g // 2, g % 2
                pe.wait_ge(masked, 8 * b.n + 2 * g + 2)
                if g == 0:
                    pe.wait_ge(v_ready, b.n + 1)
                if r == 0:
                    after(pe, u_ready, 2 * (b.n - 1) + gg + 1)
                v = v_ext[b.slot]
                for c in range(GH):
                    mm(av_bank[gg][STRIP * c:STRIP * (c + 1), 0:L], v[:, 0, r, GH * gg + c, :],
                       scores[g][:, 0:2, c, :], start=r == 0, stop=False)
                for c in range(GH):
                    last = mm(av_bank[gg][STRIP * c:STRIP * (c + 1), P:L], v[:, 1, r, GH * gg + c, :],
                              scores[g][:, 2, c, :], start=False, stop=r == 1)
                last.then_inc(av_done, 1)

            def transpose_u(b, vb):
                pe.wait_ge(u_ready, 2 * b.n + 2)
                after(pe, v_ready, upto(b.n + 2))
                for g in range(NG):
                    for j in range(NTK):
                        c = j * NG + g
                        last = transpose(p5[:, c * P:(c + 1) * P], u_sb[g][:, j * P:(j + 1) * P])
                last.then_inc(tu_done, 1)

            def transpose_xn(b):
                pe.wait_ge(xn_ready, b.n + 1)
                after(pe, x2nT_ready, b.n - 3)
                for j in range(NTK):
                    last = transpose(p6[:, j * P:(j + 1) * P], xn[:, j, :])
                last.then_inc(tn_done, 1)

            def project(b, o):
                pe.wait_ge(xnT_ready, b.n + 1)
                if o == 1:
                    after(pe, o_ready, b.n - 2)
                for g in range(NG):
                    last = mm((p6, p5)[o][:, g * L:(g + 1) * L], (wq_sb, wk_sb)[o][:, g * P:(g + 1) * P],
                              xnT[b.slot][:, :])
                last.then_inc(proj_done[o], 1)

            def project_v(b):
                after(pe, rest_ready[1], upto(b.n + 2))
                for j in range(NTK):
                    last = mm(p5[:, j * P:(j + 1) * P], xnT[b.slot][:, j * P:(j + 1) * P], wv_sb[:, :])
                last.then_inc(v_done, 1)

            def transpose_o(b):
                pe.wait_ge(o_ready, b.n + 1)
                after(pe, logit_ready, b.n)
                for j in range(NTK):
                    last = transpose(p7[:, j * P:(j + 1) * P], o_sb[:, j, :, :].rearrange("p g n -> p (g n)"))
                last.then_inc(to_done, 1)

            def project_o(b):
                pe.wait_ge(oT_ready, b.n + 1)
                for j in range(NTK):
                    last = mm(p7[:, j * P:(j + 1) * P], oT[:, j * P:(j + 1) * P], wo_sb[:, :])
                last.then_inc(wo_done, 1)

            def transpose_x2n(b):
                pe.wait_ge(x2n_ready, b.n + 1)
                after(pe, rest_ready[0], upto(b.n + 4))
                for j in range(NTK):
                    last = transpose(p6[:, j * P:(j + 1) * P], x2n[b.slot][:, j, :])
                last.then_inc(tx_done, 1)

            def gate(b):
                pe.wait_ge(x2nT_ready, b.n + 1)
                after(pe, prefix_read, b.n)
                for j in range(NTK):
                    last = mm(p7[:, j * E:(j + 1) * E], x2nT[:, j * P:(j + 1) * P], gw_sb[:, :])
                last.then_inc(gate_done, 1)

            def prefix(b):
                pe.wait_ge(onehot_ready, b.n + 1)
                after(pe, x2_ready, upto(b.n + 2))
                mm(p7[:, 0:E], before[:, :], onehot[:, 0, :])
                mm(p7[:, E:2 * E], before[:, :], onehot[:, 1, :], stop=False)
                mm(p7[:, E:2 * E], ones[:, :], onehot[:, 0, :], start=False)
                mm(p7[:, 2 * E:3 * E], ones[:, :], onehot[:, 0, :], stop=False)
                mm(p7[:, 2 * E:3 * E], ones[:, :], onehot[:, 1, :], start=False).then_inc(prefix_done, 1)

            pe.wait_ge(pool_const, 2)
            pe.wait_ge(attn_w, ATTN_WEIGHTS)

            def period(at):
                new, vb, core, tail, route = at(0), at(1), at(2), at(3), at(4)
                if core:
                    score(core, 0)
                if tail:
                    transpose_u(tail, vb)
                if new:
                    transpose_xn(new)
                if core:
                    score(core, 1)
                    weigh(core, 0)
                if tail:
                    transpose_o(tail)
                if new:
                    project(new, 0)
                if core:
                    score(core, 2)
                    weigh(core, 1)
                if tail:
                    project_o(tail)
                if new:
                    project(new, 1)
                if core:
                    score(core, 3)
                    weigh(core, 2)
                if tail:
                    transpose_x2n(tail)
                if vb:
                    project_v(vb)
                if route:
                    prefix(route)
                if core:
                    weigh(core, 3)
                if tail:
                    gate(tail)

            periods(pe, period)
            pe.wait_ge(moe_w, MOE_WEIGHTS)
            pe.wait_ge(table_ready, 1)

            def transpose_xw(t):
                pe.wait_ge(xr_in[t.slot], 16 * (t.lap + 1))
                after(pe, xwT_ready, t.n)
                transpose(xw_bank[:, 0:P], xr[t.slot][:, 0:D]).then_inc(xwt_done, 1)

            def go_up(t):
                e = pe.value_load(expert_i[0:1, bass.ds(t.n, 1)], min_val=0, max_val=E - 1)
                pe.wait_ge(xwT_ready, t.n + 1)
                after(pe, hb_ready, t.n - 1)
                mm(up_bank[t.slot % 2][:, :], xwT[t.slot % 2][:, :],
                   w1_sb[:, bass.ds(e * FF, FF)]).then_inc(up_done, 1)

            def transpose_h(t):
                pe.wait_ge(hb_ready, t.n + 1)
                after(pe, hT_ready, t.n - 1)
                for c in range(FC):
                    last = transpose(hT_bank[t.slot % 2][:, c * P:(c + 1) * P], hb[t.slot % 2][:, c * P:(c + 1) * P])
                last.then_inc(ht_done, 1)

            def go_down(t):
                e = pe.value_load(expert_i[0:1, bass.ds(t.n, 1)], min_val=0, max_val=E - 1)
                pe.wait_ge(hT_ready, t.n + 1)
                after(pe, y_ready, t.n - 1)
                for c in range(FC):
                    last = mm(down_bank[t.slot % 2][:, 0:D], hT[t.slot % 2][:, c * P:(c + 1) * P],
                              w2_sb[:, bass.ds(e * (FC * D) + c * D, D)], start=c == 0, stop=c == FC - 1)
                last.then_inc(down_done, 1)

            def step(at):
                if (t := at(0)):
                    go_up(t)
                if (t := at(1)):
                    transpose_h(t)
                if (t := at(2)):
                    go_down(t)
                if (t := at(-1)):
                    transpose_xw(t)

            transpose_xw(turn(0, RING, TILES))
            steps(pe, step)


_INS = ['L0_attn_hidden_states', 'L0_attn_Wq', 'L0_attn_Wk', 'L0_attn_Wv', 'L0_attn_Wo', 'L0_ffn_gate_w',
        'L0_ffn_gate_b', 'L0_ffn_w1', 'L0_ffn_b1', 'L0_ffn_w2', 'L0_ffn_b2']


def kernel(**inputs):
    import numpy as _np
    import concourse.bacc as _bacc
    from concourse import mybir as _mybir
    from concourse.bass_utils import run_bass_kernel_spmd as _run

    nc = _bacc.Bacc("TRN2", target_bir_lowering=False, num_devices=1)
    arrays, args = {}, []
    for name in _INS:
        a = _np.ascontiguousarray(inputs[name])
        arrays[f"in_{name}"] = a
        args.append(nc.dram_tensor(f"in_{name}", a.shape, _mybir.dt.from_np(a.dtype), kind="ExternalInput").ap())
    shape = inputs[_INS[0]].shape
    args.append(nc.dram_tensor("out_0", shape, _mybir.dt.float32, kind="ExternalOutput").ap())
    attention_moe_kernel(nc, *args)
    r = _run(nc, [arrays], core_ids=[0])
    return r.results[0]["out_0"]
```

```python
import numpy as np
import concourse.bass as bass
from concourse import mybir
from contextlib import ExitStack


class Turn:

    def __init__(self, n, lap, slot):
        self.n, self.lap, self.slot = n, lap, slot


def turn(offset, ring, total, lap=None):
    if lap is None:
        return Turn(offset, offset // ring, offset % ring) if 0 <= offset < total else None
    return Turn(lap * ring + offset, lap + offset // ring, offset % ring)


def after(engine, semaphore, count):
    if not (isinstance(count, int) and count <= 0):
        engine.wait_ge(semaphore, count)


def wait_apart(engine, semaphore, count, met):
    if not isinstance(count, int):
        count = engine.to_reg(count)
    engine.wait_ge(*met)
    engine.wait_ge(semaphore, count)


def attention_moe_kernel(nc, x, Wq, Wk, Wv, Wo, gate_w, gate_b, w1, b1, w2, b2, out):
    fp32 = mybir.dt.float32
    bf16 = mybir.dt.bfloat16
    i32 = mybir.dt.int32
    ALU = mybir.AluOpType
    ACT = mybir.ActivationFunctionType
    AX = mybir.AxisListType

    NB, L, D = x.shape
    P = 128
    NTK = L // P
    H, F, HD = 16, 16, 8
    E, _, FF = w1.shape
    FC = FF // P
    TOK = NB * L
    LN_EPS = 1e-5
    ATT_EPS = 1e-5
    TINY = 1e-30
    Q_SCALE = float(F) ** -0.5

    HG = P // F
    NG = H // HG
    PARTS = 3
    K_SLOTS = (0, 0, 0, 1, 1, 2)
    Q_SLOTS = (0, 1, 2, 0, 1, 0)
    SLOTS = len(K_SLOTS)
    KS = SLOTS * F
    GROUPS = 4
    GH = H // GROUPS
    STRIP = 32
    SUB = 16

    REGION = TOK + P
    ROWW = 2 * D + 4
    IDCOL = 2 * D
    NOWHERE = TOK
    TILES = TOK // P + E - 1
    RING = 4

    region = nc.dram_tensor("expert_rows", (E * REGION + P, ROWW), fp32, kind="Internal").ap()
    scratch = nc.dram_tensor("qk_parts", (2, 2, PARTS, H, F, L), bf16, kind="Internal").ap()

    ctx = ExitStack()
    with ctx:
        def sb(name, shape, dt=fp32):
            return ctx.enter_context(nc.sbuf_tensor(name, shape, dt))

        def sem(name):
            return ctx.enter_context(nc.semaphore(name))

        wq_sb = sb("wq_sb", [P, H * F])
        wk_sb = sb("wk_sb", [P, H * F])
        wv_sb = sb("wv_sb", [P, H * HD])
        wo_sb = sb("wo_sb", [P, D])
        gw_sb = sb("gw_sb", [P, E])
        gb_sb = sb("gb_sb", [P, E])
        w1_sb = sb("w1_sb", [P, E * FF])
        w2_sb = sb("w2_sb", [P, E * FC * D])
        b1_sb = sb("b1_sb", [P, E * FF])
        b2_sb = sb("b2_sb", [P, E * D])
        ident = sb("ident", [P, P])
        before = sb("before", [P, P], bf16)
        ones = sb("ones", [P, P], bf16)
        minus_half = sb("minus_half", [P, NTK])
        number1_i = sb("number1_i", [P, E], i32)
        number1 = sb("number1", [P, E])
        ties = sb("ties", [P, E, E])
        token_i = sb("token_i", [P, NTK], i32)
        token = sb("token", [P, NTK])
        base = sb("base", [P, E])
        pad_rows = sb("pad_rows", [P, ROWW])
        tile_i = sb("tile_i", [1, TILES], i32)
        tile_no = sb("tile_no", [1, TILES])

        x_ln = [sb(f"x_ln{i}", [P, NTK, D]) for i in range(2)]
        x_res = [sb(f"x_res{i}", [P, NTK, D]) for i in range(2)]
        stats1 = sb("stats1", [P, NTK, 6])
        mv1 = sb("mv1", [P, NTK, 2])
        ve1 = sb("ve1", [P, NTK])
        rstd1 = sb("rstd1", [P, NTK])
        xn = sb("xn", [P, NTK, D])
        xnT = [sb(f"xnT{i}", [P, L]) for i in range(2)]
        parts = [[sb(f"parts{o}{i}", [P, PARTS, NG * L], bf16) for i in range(2)] for o in range(2)]
        rest = [sb(f"rest{o}", [P, NG * L]) for o in range(2)]
        stack = [[sb(f"stack{o}{i}", [KS, H, L], bf16) for i in range(2)] for o in range(2)]
        v_ext = [sb(f"v_ext{i}", [P, NTK, 2, H // 2, STRIP]) for i in range(2)]
        scores = [sb(f"scores{g}", [P, 3, GH, P]) for g in range(GROUPS)]
        u_sb = [sb(f"u_sb{g}", [P, L]) for g in range(NG)]
        den = sb("den", [P, NG * NTK, HG])
        rden = sb("rden", [P, NG * NTK, HG])
        o_sb = sb("o_sb", [P, NTK, NG, HG * HD])
        oT = sb("oT", [P, L])

        row = [sb(f"row{i}", [P, NTK, ROWW]) for i in range(2)]
        stats2 = sb("stats2", [P, NTK, 6])
        mv2 = sb("mv2", [P, NTK, 2])
        ve2 = sb("ve2", [P, NTK])
        rstd2 = sb("rstd2", [P, NTK])
        x2n = [sb(f"x2n{i}", [P, NTK, D]) for i in range(2)]
        x2nT = sb("x2nT", [P, L])
        logit = sb("logit", [P, NTK, E])
        top = sb("top", [P, NTK])
        shifted = sb("shifted", [P, NTK, E])
        expo = sb("expo", [P, NTK, E])
        esum = sb("esum", [P, NTK])
        rsum = sb("rsum", [P, NTK])
        score = sb("score", [P, NTK, E])
        gap = sb("gap", [P, NTK, E, E])
        ahead = sb("ahead", [P, NTK, E, E])
        rank = sb("rank", [P, NTK, E])
        key0 = sb("key0", [P, NTK, E])
        key = sb("key", [P, NTK, E])
        chosen = sb("chosen", [P, NTK])
        onehot = sb("onehot", [P, NTK, E], bf16)
        picked = sb("picked", [P, NTK, E])
        weight = sb("weight", [P, NTK])
        place = sb("place", [P, NTK, E])
        placed = sb("placed", [P, NTK, E])
        nth = sb("nth", [P, NTK])
        slot_i = [sb(f"slot_i{i}", [P, NTK], i32) for i in range(2)]

        count = sb("count", [1, E])
        count_i = sb("count_i", [1, E], i32)
        ntile_f = sb("ntile_f", [1, E])
        ntile_i = sb("ntile_i", [1, E], i32)
        cum = [sb(f"cum{i}", [1, E]) for i in range(4)]
        passed = sb("passed", [1, TILES, E])
        tile_e = sb("tile_e", [1, TILES])
        passed_c = sb("passed_c", [1, TILES, E])
        first = sb("first", [1, TILES])
        local = sb("local", [1, TILES])
        e_row = sb("e_row", [1, TILES])
        t_row = sb("t_row", [1, TILES])
        row_i = sb("row_i", [1, TILES], i32)
        expert_i = sb("expert_i", [1, TILES], i32)

        xr = [sb(f"xr{i}", [P, ROWW]) for i in range(RING)]
        xwT = [sb(f"xwT{i}", [P, P]) for i in range(2)]
        hb = [sb(f"hb{i}", [P, FF]) for i in range(2)]
        hT = [sb(f"hT{i}", [P, FF]) for i in range(2)]
        x2b = [sb(f"x2b{i}", [P, D]) for i in range(2)]
        token_of = [sb(f"token_of{i}", [P, 1], i32) for i in range(RING)]
        y_sb = [sb(f"y_sb{i}", [P, D]) for i in range(RING)]

        bank = [ctx.enter_context(nc.psum_tensor(f"bank{i}", [P, 512], fp32)) for i in range(8)]
        score_bank = bank[0:3]
        av_bank = bank[3:5]
        prefix_bank = av_bank[1]
        p5, p6, p7 = bank[5], bank[6], bank[7]
        up_bank = bank[0:2]
        xw_bank = bank[2]
        hT_bank = bank[3:5]
        down_bank = bank[5:7]

        attn_w = sem("attn_w")
        moe_w = sem("moe_w")
        pads_in = sem("pads_in")
        pool_const = sem("pool_const")
        pool_step = sem("pool_step")
        dve_const = sem("dve_const")
        x_ln_in = [sem(f"x_ln_in{i}") for i in range(2)]
        x_res_in = [sem(f"x_res_in{i}") for i in range(2)]
        ln1_step = sem("ln1_step")
        ln1_stats = sem("ln1_stats")
        ln1_var = sem("ln1_var")
        ln1_rstd = sem("ln1_rstd")
        xn_ready = sem("xn_ready")
        tn_done = sem("tn_done")
        xnT_ready = sem("xnT_ready")
        proj_done = [sem("q_done"), sem("k_done")]
        high_ready = [sem("q_high"), sem("k_high")]
        rest_ready = [sem("q_rest"), sem("k_rest")]
        mid_ready = [sem("q_mid"), sem("k_mid")]
        low_ready = [sem("q_low"), sem("k_low")]
        parts_out = [sem(f"parts_out{i}") for i in range(2)]
        stack_in = [sem(f"stack_in{i}") for i in range(2)]
        v_done = sem("v_done")
        v_ready = sem("v_ready")
        scored = sem("scored")
        squared = sem("squared")
        masked = sem("masked")
        av_done = sem("av_done")
        u_ready = sem("u_ready")
        tu_done = sem("tu_done")
        den_step = sem("den_step")
        o_ready = sem("o_ready")
        to_done = sem("to_done")
        oT_ready = sem("oT_ready")
        wo_done = sem("wo_done")
        x2_ready = sem("x2_ready")
        ln2_step = sem("ln2_step")
        ln2_stats = sem("ln2_stats")
        ln2_var = sem("ln2_var")
        ln2_rstd = sem("ln2_rstd")
        x2n_ready = sem("x2n_ready")
        tx_done = sem("tx_done")
        x2nT_ready = sem("x2nT_ready")
        gate_done = sem("gate_done")
        logit_ready = sem("logit_ready")
        gap_ready = sem("gap_ready")
        top_ready = sem("top_ready")
        shifted_ready = sem("shifted_ready")
        expo_ready = sem("expo_ready")
        route_step = sem("route_step")
        onehot_ready = sem("onehot_ready")
        prefix_done = sem("prefix_done")
        prefix_read = sem("prefix_read")
        row_ready = sem("row_ready")
        rows_out = [sem(f"rows_out{i}") for i in range(2)]
        table_step = sem("table_step")
        counts_ready = sem("counts_ready")
        table_ready = sem("table_ready")
        xr_in = [sem(f"xr_in{i}") for i in range(RING)]
        xwt_done = sem("xwt_done")
        xwT_ready = sem("xwT_ready")
        up_done = sem("up_done")
        hb_ready = sem("hb_ready")
        ht_done = sem("ht_done")
        hT_ready = sem("hT_ready")
        down_done = sem("down_done")
        x2b_ready = sem("x2b_ready")
        y_ready = sem("y_ready")
        y_out = [sem(f"y_out{i}") for i in range(RING)]

        ROUTE_STEPS = 12
        consts = (pool_const, 2)
        ATTN_WEIGHTS = 6 * 16
        MOE_WEIGHTS = 4 * 16

        PERIODS = NB + 5
        LOOP_FROM, LOOP_LAPS = 5, (NB - 7) // 2

        def periods(engine, period):
            def item_at(p, lap=None):
                return lambda lag, total=NB: turn(p - lag, 2, total, lap)

            for p in range(-1, LOOP_FROM):
                period(item_at(p))
            with engine.Fori(0, LOOP_LAPS) as lap:
                for p in range(LOOP_FROM, LOOP_FROM + 2):
                    period(item_at(p, lap))
            for p in range(LOOP_FROM + 2 * LOOP_LAPS, PERIODS):
                period(item_at(p))

        def upto(count):
            return min(count, NB) if isinstance(count, int) else count

        def steps(engine, step):
            def item_at(s, lap=None):
                return lambda lag: turn(s - lag, RING, TILES, lap)

            laps = (TILES - 3 - RING) // RING
            for s in range(RING):
                step(item_at(s))
            with engine.Fori(0, laps) as lap:
                for s in range(RING, 2 * RING):
                    step(item_at(s, lap))
            for s in range(RING + RING * laps, TILES + 2):
                step(item_at(s))

        def pad_experts(engine, half):
            engine.wait_ge(counts_ready, 1)
            engine.wait_ge(pool_const, 1)
            for e in range(half, E, 2):
                n = engine.value_load(count_i[0:1, e:e + 1], min_val=0, max_val=TOK)
                engine.dma_start(region[bass.ds(n + e * REGION, P), :], pad_rows[:, :]).then_inc(pads_in, 16)

        block = ctx.enter_context(nc.Block())

        @block.sync
        def _(sp):
            def load_stacks(b):
                after(sp, parts_out[b.slot], 32 * (b.lap + 1))
                after(sp, scored, 12 * (b.n - 1))
                for o, slots in ((0, Q_SLOTS), (1, K_SLOTS)):
                    for s, part in enumerate(slots):
                        sp.dma_start(stack[o][b.slot][F * s:F * (s + 1), :, :],
                                     scratch[b.slot, o, part].rearrange("h f t -> f h t")
                                     ).then_inc(stack_in[b.slot], 16)

            def load_x(b):
                after(sp, xn_ready, b.n - 1)
                sp.dma_start(x_ln[b.slot][:, :, :], x_tiles(b)).then_inc(x_ln_in[b.slot], 16)

            def load_residual(b):
                after(sp, x2_ready, b.n - 1)
                sp.dma_start(x_res[b.slot][:, :, :], x_tiles(b)).then_inc(x_res_in[b.slot], 16)

            def x_tiles(b):
                return x[bass.ds(b.n, 1)].rearrange("a (j p) d -> p (a j) d", p=P)

            def store_parts(b, o):
                wait_apart(sp, low_ready[o], b.n + 1, consts)
                if o == 0:
                    after(sp, stack_in[b.slot], 16 * 2 * SLOTS * b.lap)
                sp.dma_start(scratch[b.slot, o].rearrange("a (g h) f t -> (h f) a g t", g=NG),
                             parts[o][b.slot][:, :, :].rearrange("p a (g t) -> p a g t", g=NG)
                             ).then_inc(parts_out[b.slot], 16)

            for dst, src in ((wq_sb, Wq), (wk_sb, Wk), (wv_sb, Wv), (wo_sb, Wo), (gw_sb, gate_w)):
                if dst is wq_sb:
                    load_x(turn(0, 2, NB))
                sp.dma_start(dst[:, :], src).then_inc(attn_w, 16)
            sp.dma_start(gb_sb[:, :], gate_b.partition_broadcast(P)).then_inc(attn_w, 16)

            def period(at):
                if (b := at(1)):
                    load_stacks(b)
                if (b := at(-2)):
                    load_x(b)
                if (b := at(3)):
                    load_residual(b)
                if (b := at(0)):
                    store_parts(b, 0)
                    store_parts(b, 1)

            periods(sp, period)

            pad_experts(sp, 0)
            for i in range(2):
                sp.wait_ge(rows_out[i], 16 * NTK * (NB // 2))
            sp.wait_ge(pads_in, 16 * (E + 1))
            sp.wait_ge(table_ready, 1)

            def load_tile(t):
                after(sp, xwt_done, t.n - RING + 1)
                after(sp, x2b_ready, t.n - RING + 1)
                at_row = sp.value_load(row_i[0:1, bass.ds(t.n, 1)], min_val=0, max_val=E * REGION)
                sp.dma_start(xr[t.slot][:, :], region[bass.ds(at_row, P), :]).then_inc(xr_in[t.slot], 16)

            for s in range(RING):
                load_tile(turn(s, RING, TILES))
            with sp.Fori(0, TILES // RING - 1) as lap:
                for s in range(RING, 2 * RING):
                    load_tile(turn(s, RING, TILES, lap))
            for s in range(TILES // RING * RING, TILES):
                load_tile(turn(s, RING, TILES))
            for i in range(RING):
                sp.wait_ge(y_out[i], 16 * ((TILES - 1 - i) // RING + 1))

        @block.scalar
        def _(act):
            act.wait_ge(pool_const, 1)
            act.dma_start(region[E * REGION:E * REGION + P, :], pad_rows[:, :]).then_inc(pads_in, 16)

            def load_experts(p):
                if p == 1:
                    act.dma_start(w1_sb[:, :].rearrange("p (e n) -> p e n", e=E),
                                  w1.rearrange("e d n -> d e n")).then_inc(moe_w, 16)
                if p == 2:
                    act.dma_start(w2_sb[:, :].rearrange("p (e c n) -> p e c n", e=E, c=FC),
                                  w2.rearrange("e (c f) n -> f e c n", c=FC)).then_inc(moe_w, 16)
                if p == 3:
                    act.dma_start(b1_sb[:, :], b1.rearrange("e n -> (e n)").partition_broadcast(P)
                                  ).then_inc(moe_w, 16)
                if p == 4:
                    act.dma_start(b2_sb[:, :], b2.rearrange("e n -> (e n)").partition_broadcast(P)
                                  ).then_inc(moe_w, 16)

            def square(b, g):
                for k in range(3):
                    act.wait_ge(scored, 12 * b.n + 3 * g + k + 1)
                    if k == 0:
                        after(act, av_done, GROUPS * (b.n - 1) + g + 1)
                    nc.scalar.activation(scores[g][:, k, :, :].rearrange("p h t -> p (h t)"),
                                         score_bank[k][:, :], ACT.Square, scale=Q_SCALE).then_inc(squared, 1)

            def exponent(b):
                act.wait_ge(shifted_ready, b.n + 1)
                after(act, onehot_ready, b.n)
                nc.scalar.activation(expo[:, :, :], shifted[:, :, :], ACT.Exp).then_inc(expo_ready, 1)

            def copy_xnT(b):
                act.wait_ge(tn_done, b.n + 1)
                after(act, v_done, b.n - 1)
                nc.scalar.copy(xnT[b.slot][:, :], p6[:, 0:L]).then_inc(xnT_ready, 1)

            def high(b, o):
                act.wait_ge(proj_done[o], b.n + 1)
                after(act, parts_out[b.slot], 32 * b.lap)
                nc.scalar.copy(parts[o][b.slot][:, 0, :], (p6, p5)[o][:, :]).then_inc(high_ready[o], 1)

            def middle(b, o):
                act.wait_ge(rest_ready[o], b.n + 1)
                nc.scalar.copy(parts[o][b.slot][:, 1, :], rest[o][:, :]).then_inc(mid_ready[o], 1)

            def copy_u(b, g):
                act.wait_ge(av_done, GROUPS * b.n + 2 * g + 2)
                after(act, tu_done, b.n)
                nc.scalar.copy(u_sb[g][:, :], av_bank[g][:, 0:L]).then_inc(u_ready, 1)

            def copy_oT(b):
                act.wait_ge(to_done, b.n + 1)
                after(act, wo_done, b.n)
                nc.scalar.copy(oT[:, :], p7[:, 0:L]).then_inc(oT_ready, 1)

            def copy_x2nT(b):
                act.wait_ge(tx_done, b.n + 1)
                after(act, gate_done, b.n)
                nc.scalar.copy(x2nT[:, :], p6[:, 0:L]).then_inc(x2nT_ready, 1)

            def period(at):
                new, core, late, tail, route, nxt = at(0), at(2), at(3), at(4), at(5), at(-1)
                if core:
                    square(core, 0)
                if new:
                    high(new, 0)
                if route:
                    exponent(route)
                if core:
                    square(core, 1)
                if late:
                    copy_u(late, 1)
                if new:
                    middle(new, 0)
                    high(new, 1)
                if core:
                    square(core, 2)
                if new:
                    middle(new, 1)
                if tail:
                    copy_x2nT(tail)
                if core:
                    square(core, 3)
                if nxt:
                    copy_xnT(nxt)
                if late:
                    copy_oT(late)
                if core:
                    copy_u(core, 0)
                if new and isinstance(new.n, int):
                    load_experts(new.n)

            periods(act, period)

            def step(at):
                if (t := at(-1)):
                    copy_xwT(t)
                if (t := at(1)):
                    act.wait_ge(ht_done, t.n + 1)
                    after(act, down_done, t.n - 1)
                    nc.scalar.activation(hT[t.slot % 2][:, :], hT_bank[t.slot % 2][:, :],
                                         ACT.Relu).then_inc(hT_ready, 1)

            def copy_xwT(t):
                act.wait_ge(xwt_done, t.n + 1)
                after(act, up_done, t.n - 1)
                nc.scalar.copy(xwT[t.slot % 2][:, :], xw_bank[:, 0:P]).then_inc(xwT_ready, 1)

            pad_experts(act, 1)
            copy_xwT(turn(0, RING, TILES))
            steps(act, step)

        @block.gpsimd
        def _(pool):
            nc.gpsimd.memset(pad_rows[:, :], 0.0).then_inc(pool_step, 1)
            nc.gpsimd.memset(ident[:, :], 0.0)
            nc.gpsimd.memset(before[:, :], 1.0)
            nc.gpsimd.memset(ones[:, :], 1.0)
            nc.gpsimd.memset(minus_half[:, :], -0.5)
            nc.gpsimd.memset(ties[:, :, :], -TINY)
            nc.gpsimd.memset(base[:, :], -float(REGION)).then_inc(pool_step, 1)
            pool.wait_ge(pool_step, 2)
            nc.gpsimd.memset(pad_rows[:, IDCOL:IDCOL + 1].bitcast(i32), NOWHERE).then_inc(pool_const, 1)
            nc.gpsimd.affine_select(out=ident[:, :], in_=ident[:, :], compare_op=ALU.not_equal, fill=1.0,
                                    base=0, pattern=[[-1, P]], channel_multiplier=1)
            nc.gpsimd.affine_select(out=before[:, :], in_=before[:, :], compare_op=ALU.is_gt, fill=0.0,
                                    base=0, pattern=[[1, P]], channel_multiplier=-1)
            nc.gpsimd.affine_select(out=ties[:, :, :], in_=ties[:, :, :], compare_op=ALU.is_gt, fill=TINY,
                                    base=0, pattern=[[1, E], [-1, E]], channel_multiplier=0)
            nc.gpsimd.iota(number1_i[:, :], pattern=[[1, E]], base=1, channel_multiplier=0)
            nc.gpsimd.iota(tile_i[:, :], pattern=[[1, TILES]], base=0, channel_multiplier=0)
            nc.gpsimd.iota(token_i[:, :], pattern=[[P, NTK]], base=0, channel_multiplier=1).then_inc(pool_step, 1)
            pool.wait_ge(pool_step, 3)
            nc.gpsimd.tensor_copy(number1[:, :], number1_i[:, :])
            nc.gpsimd.tensor_copy(tile_no[:, :], tile_i[:, :])
            nc.gpsimd.tensor_copy(token[:, :], token_i[:, :]).then_inc(pool_const, 1)

            def mask(b, g):
                for k, of in ((0, 1), (2, 3)):
                    wait_apart(pool, squared, 12 * b.n + 3 * g + of, consts)
                    nc.gpsimd.affine_select(out=scores[g][:, k, :, :], in_=scores[g][:, k, :, :],
                                            compare_op=ALU.is_ge, fill=0.0, base=0,
                                            pattern=[[0, GH], [1, P]], channel_multiplier=-1).then_inc(masked, 1)

            def reciprocal_root(b, mv, ve, rstd, stats, var, done):
                wait_apart(pool, stats, b.n + 1, consts)
                nc.gpsimd.tensor_scalar_add(ve[:, :], mv[:, :, 1], LN_EPS).then_inc(var, 1)
                pool.wait_ge(var, b.n + 1)
                nc.gpsimd.tensor_tensor(rstd[:, :], ve[:, :], minus_half[:, :], ALU.pow).then_inc(done, 1)

            def compare(b):
                pool.wait_ge(logit_ready, b.n + 1)
                after(pool, onehot_ready, b.n)
                for j in range(NTK):
                    last = nc.gpsimd.tensor_tensor(gap[:, j, :, :], logit[:, j, :].unsqueeze(1).broadcast_to([P, E, E]),
                                                   logit[:, j, :].unsqueeze(2).broadcast_to([P, E, E]), ALU.subtract)
                last.then_inc(gap_ready, 1)

            def scatter(b):
                wait_apart(pool, row_ready, b.n + 1, consts)
                for j in range(NTK):
                    nc.gpsimd.indirect_dma_start(
                        out=region, out_offset=bass.IndirectOffsetOnAxis(ap=slot_i[b.slot][:, j:j + 1], axis=0),
                        in_=row[b.slot][:, j, :], in_offset=None).then_inc(rows_out[b.slot], 16)

            def norm1(b):
                reciprocal_root(b, mv1, ve1, rstd1, ln1_stats, ln1_var, ln1_rstd)

            def period(at):
                core, tail, route, nxt = at(2), at(4), at(5), at(-1)
                if core:
                    mask(core, 0)
                if route:
                    compare(route)
                if tail:
                    reciprocal_root(tail, mv2, ve2, rstd2, ln2_stats, ln2_var, ln2_rstd)
                if nxt:
                    norm1(nxt)
                if core:
                    mask(core, 1)
                    mask(core, 2)
                if route:
                    scatter(route)
                if core:
                    mask(core, 3)

            periods(pool, period)
            pool.wait_ge(moe_w, MOE_WEIGHTS)
            pool.wait_ge(table_ready, 1)

            def add_bias(t):
                e = pool.value_load(expert_i[0:1, bass.ds(t.n, 1)], min_val=0, max_val=E - 1)
                pool.wait_ge(xr_in[t.slot], 16 * (t.lap + 1))
                after(pool, y_ready, t.n - 1)
                nc.gpsimd.tensor_tensor(x2b[t.slot % 2][:, :], xr[t.slot][:, D:2 * D],
                                        b2_sb[:, bass.ds(e * D, D)], ALU.add)
                if not isinstance(t.lap, int) or t.lap:
                    wait_apart(pool, y_out[t.slot], 16 * t.lap, consts)
                nc.gpsimd.tensor_copy(token_of[t.slot][:, :],
                                      xr[t.slot][:, IDCOL:IDCOL + 1].bitcast(i32)).then_inc(x2b_ready, 1)

            def scatter_out(t):
                wait_apart(pool, y_ready, t.n + 1, consts)
                nc.gpsimd.indirect_dma_start(
                    out=out.rearrange("b l d -> (b l) d"),
                    out_offset=bass.IndirectOffsetOnAxis(ap=token_of[t.slot][:, 0:1], axis=0),
                    in_=y_sb[t.slot][:, :], in_offset=None,
                    bounds_check=TOK - 1, oob_is_err=False).then_inc(y_out[t.slot], 16)

            def step(at):
                if (t := at(0)):
                    add_bias(t)
                if (t := at(2)):
                    scatter_out(t)

            steps(pool, step)

        @block.vector
        def _(dve):
            for i in range(2):
                nc.vector.memset(v_ext[i][:, :, :, :, :], 0.0)
                nc.vector.memset(row[i][:, :, :], 0.0).then_inc(dve_const, 1)
            dve.wait_ge(dve_const, 2)
            for i in range(2):
                for r in range(2):
                    nc.vector.memset(v_ext[i][:, :, r, :, SUB * r + HD:SUB * r + HD + 1], 1.0)
            dve.wait_ge(pool_const, 2)

            def norm_stats(b, src, stats, mv, step, done):
                for j in range(NTK):
                    ins = nc.vector.bn_stats(stats[:, j, :], src[:, j, :])
                ins.then_inc(step, 1)
                wait_apart(dve, step, b.n + 1, consts)
                for j in range(NTK):
                    ins = nc.vector.bn_aggr(mv[:, j, :], stats[:, j, :])
                ins.then_inc(done, 1)

            def norm1_stats(b):
                dve.wait_ge(x_ln_in[b.slot], 16 * (b.lap + 1))
                norm_stats(b, x_ln[b.slot], stats1, mv1, ln1_step, ln1_stats)

            def norm1_apply(b):
                dve.wait_ge(ln1_rstd, b.n + 1)
                after(dve, tn_done, b.n)
                for j in range(NTK):
                    ins = nc.vector.tensor_scalar(xn[:, j, :], x_ln[b.slot][:, j, :], mv1[:, j, 0:1],
                                                  rstd1[:, j:j + 1], ALU.subtract, ALU.mult)
                ins.then_inc(xn_ready, 1)

            def split(b, o):
                dve.wait_ge(high_ready[o], b.n + 1)
                nc.vector.tensor_tensor(rest[o][:, :], (p6, p5)[o][:, :], parts[o][b.slot][:, 0, :],
                                        ALU.subtract).then_inc(rest_ready[o], 1)

            def low(b, o):
                dve.wait_ge(mid_ready[o], b.n + 1)
                nc.vector.tensor_tensor(parts[o][b.slot][:, 2, :], rest[o][:, :], parts[o][b.slot][:, 1, :],
                                        ALU.subtract).then_inc(low_ready[o], 1)

            def place_v(b):
                dve.wait_ge(v_done, b.n + 1)
                after(dve, av_done, GROUPS * (b.n - 1))
                for r in range(2):
                    ins = nc.vector.tensor_copy(
                        v_ext[b.slot][:, :, r, :, SUB * r:SUB * r + HD],
                        p5[:, 0:NTK * H * HD].rearrange("p (j x r d) -> p j x r d", j=NTK, r=2, d=HD)[:, :, :, r, :])
                ins.then_inc(v_ready, 1)

            def divide(b):
                dve.wait_ge(tu_done, b.n + 1)
                heads = p5[:, :].rearrange("p (j h w) -> p j h w", h=HG, w=SUB)
                nc.vector.tensor_scalar_add(den[:, :, :], heads[:, :, :, HD], ATT_EPS).then_inc(den_step, 1)
                dve.wait_ge(den_step, 2 * b.n + 1)
                nc.vector.reciprocal(rden[:, :, :], den[:, :, :]).then_inc(den_step, 1)
                dve.wait_ge(den_step, 2 * b.n + 2)
                after(dve, to_done, b.n)
                nc.vector.tensor_tensor(o_sb[:, :, :, :].rearrange("p j g (h d) -> p (j g) h d", d=HD),
                                        heads[:, :, :, 0:HD],
                                        rden[:, :, :].unsqueeze(3).broadcast_to([P, NG * NTK, HG, HD]),
                                        ALU.mult).then_inc(o_ready, 1)

            def residual(b):
                dve.wait_ge(wo_done, b.n + 1)
                dve.wait_ge(x_res_in[b.slot], 16 * (b.lap + 1))
                after(dve, rows_out[b.slot], 16 * NTK * b.lap)
                nc.vector.tensor_tensor(row[b.slot][:, :, D:2 * D],
                                        p7[:, 0:NTK * D].rearrange("p (j d) -> p j d", j=NTK),
                                        x_res[b.slot][:, :, :], ALU.add).then_inc(x2_ready, 1)
                dve.wait_ge(x2_ready, b.n + 1)
                norm_stats(b, row[b.slot][:, :, D:2 * D], stats2, mv2, ln2_step, ln2_stats)

            def norm2_apply(b):
                dve.wait_ge(ln2_rstd, b.n + 1)
                after(dve, tx_done, b.n - 1)
                for j in range(NTK):
                    ins = nc.vector.tensor_scalar(x2n[b.slot][:, j, :], row[b.slot][:, j, D:2 * D],
                                                  mv2[:, j, 0:1], rstd2[:, j:j + 1], ALU.subtract, ALU.mult)
                ins.then_inc(x2n_ready, 1)

            def wide(ap):
                return ap.unsqueeze(2).broadcast_to([P, NTK, E])

            def shared(ap):
                return ap.unsqueeze(1).broadcast_to([P, NTK, E])

            def route_logits(b):
                dve.wait_ge(gate_done, b.n + 1)
                nc.vector.tensor_tensor(logit[:, :, :], p7[:, 0:NTK * E].rearrange("p (j e) -> p j e", j=NTK),
                                        shared(gb_sb[:, :]), ALU.add).then_inc(logit_ready, 1)
                dve.wait_ge(logit_ready, b.n + 1)
                nc.vector.reduce_max(top[:, :], logit[:, :, :], AX.X).then_inc(top_ready, 1)
                dve.wait_ge(top_ready, b.n + 1)
                nc.vector.tensor_tensor(shifted[:, :, :], logit[:, :, :], wide(top[:, :]),
                                        ALU.subtract).then_inc(shifted_ready, 1)

            def stepped(b, k, ins):
                ins.then_inc(route_step, 1)
                dve.wait_ge(route_step, ROUTE_STEPS * b.n + k)

            def route_choice(b):
                dve.wait_ge(expo_ready, b.n + 1)
                stepped(b, 1, nc.vector.reduce_sum(esum[:, :], expo[:, :, :], AX.X))
                stepped(b, 2, nc.vector.reciprocal(rsum[:, :], esum[:, :]))
                stepped(b, 3, nc.vector.tensor_tensor(score[:, :, :], expo[:, :, :], wide(rsum[:, :]), ALU.mult))
                stepped(b, 4, nc.vector.scalar_tensor_tensor(out=key0[:, :, :], in0=score[:, :, :], scalar=0.0,
                                                          in1=shared(number1[:, :]), op0=ALU.is_gt, op1=ALU.mult))
                dve.wait_ge(gap_ready, b.n + 1)
                stepped(b, 5, nc.vector.tensor_tensor(ahead[:, :, :, :], gap[:, :, :, :],
                                                   ties[:, :, :].unsqueeze(1).broadcast_to([P, NTK, E, E]),
                                                   ALU.is_ge))
                stepped(b, 6, nc.vector.reduce_sum(rank[:, :, :], ahead[:, :, :, :], AX.X))
                stepped(b, 7, nc.vector.scalar_tensor_tensor(out=key[:, :, :], in0=rank[:, :, :], scalar=1.5,
                                                          in1=key0[:, :, :], op0=ALU.is_lt, op1=ALU.mult))
                stepped(b, 8, nc.vector.reduce_max(chosen[:, :], key[:, :, :], AX.X))
                after(dve, prefix_done, b.n)
                nc.vector.tensor_tensor(onehot[:, :, :], key[:, :, :], wide(chosen[:, :]),
                                        ALU.is_equal).then_inc(onehot_ready, 1)

            def route_place(b):
                dve.wait_ge(prefix_done, b.n + 1)
                nc.vector.tensor_tensor(place[:, :, :], prefix_bank[:, 0:NTK * E].rearrange("p (j e) -> p j e", j=NTK),
                                        shared(base[:, :]), ALU.add).then_inc(route_step, 1)
                dve.wait_ge(route_step, ROUTE_STEPS * b.n + 9)
                nc.vector.tensor_tensor(base[:, :], base[:, :], prefix_bank[:, NTK * E:(NTK + 1) * E],
                                        ALU.add).then_inc(prefix_read, 1)
                nc.vector.tensor_tensor(picked[:, :, :], onehot[:, :, :], score[:, :, :], ALU.mult)
                stepped(b, 10, nc.vector.tensor_tensor(placed[:, :, :], onehot[:, :, :], place[:, :, :], ALU.mult))
                nc.vector.reduce_sum(weight[:, :], picked[:, :, :], AX.X)
                stepped(b, 11, nc.vector.reduce_sum(nth[:, :], placed[:, :, :], AX.X))
                nc.vector.scalar_tensor_tensor(out=slot_i[b.slot][:, :], in0=chosen[:, :], scalar=float(REGION),
                                               in1=nth[:, :], op0=ALU.mult, op1=ALU.add)

            def route_row(b):
                for j in range(NTK):
                    nc.vector.tensor_scalar(row[b.slot][:, j, 0:D], x2n[b.slot][:, j, :], weight[:, j:j + 1], None,
                                            ALU.mult)
                nc.vector.tensor_copy(row[b.slot][:, :, IDCOL].bitcast(i32), token[:, :]).then_inc(row_ready, 1)
                stepped(b, 12, nc.vector.tensor_scalar_add(token[:, :], token[:, :], float(L)))

            def period(at):
                new, vb, late, tail, route, nxt = at(0), at(1), at(3), at(4), at(5), at(-1)
                if route and not late:
                    route_choice(route)
                if new:
                    split(new, 0)
                if tail:
                    residual(tail)
                if nxt:
                    norm1_stats(nxt)
                if new:
                    low(new, 0)
                    split(new, 1)
                if tail:
                    norm2_apply(tail)
                if route and late:
                    route_choice(route)
                if nxt:
                    norm1_apply(nxt)
                if new:
                    low(new, 1)
                if late:
                    divide(late)
                if route:
                    route_place(route)
                if tail:
                    route_logits(tail)
                if vb:
                    place_v(vb)
                if route:
                    route_row(route)

            periods(dve, period)

            ts = [0]

            def tabled(ins):
                ts[0] += 1
                ins.then_inc(table_step, 1)
                dve.wait_ge(table_step, ts[0])

            dve.wait_ge(prefix_read, NB)
            tabled(nc.vector.tensor_scalar_add(count[:, :], base[0:1, :], float(REGION)))
            nc.vector.tensor_copy(count_i[:, :], count[:, :]).then_inc(counts_ready, 1)
            tabled(nc.vector.tensor_scalar(ntile_f[:, :], count[:, :], 1.0 / P,
                                            (P - 1) / P - 0.5 + 0.5 / P, ALU.mult, ALU.add))
            tabled(nc.vector.tensor_copy(ntile_i[:, :], ntile_f[:, :]))
            tabled(nc.vector.tensor_copy(cum[0][:, :], ntile_i[:, :]))
            for k in range(3):
                d = 1 << k
                nc.vector.tensor_copy(cum[k + 1][:, 0:d], cum[k][:, 0:d])
                tabled(nc.vector.tensor_tensor(cum[k + 1][:, d:E], cum[k][:, d:E], cum[k][:, 0:E - d], ALU.add))
            per_tile = cum[3][:, :].unsqueeze(1).broadcast_to([1, TILES, E])
            tabled(nc.vector.tensor_tensor(passed[:, :, :],
                                            tile_no[:, :].unsqueeze(2).broadcast_to([1, TILES, E]),
                                            per_tile, ALU.is_ge))
            nc.vector.reduce_sum(tile_e[:, :], passed[:, :, :], AX.X)
            tabled(nc.vector.tensor_tensor(passed_c[:, :, :], passed[:, :, :], per_tile, ALU.mult))
            tabled(nc.vector.reduce_max(first[:, :], passed_c[:, :, :], AX.X))
            nc.vector.tensor_tensor(local[:, :], tile_no[:, :], first[:, :], ALU.subtract)
            tabled(nc.vector.tensor_scalar(e_row[:, :], tile_e[:, :], float(REGION), None, ALU.mult))
            tabled(nc.vector.scalar_tensor_tensor(out=t_row[:, :], in0=local[:, :], scalar=float(P),
                                                   in1=e_row[:, :], op0=ALU.mult, op1=ALU.add))
            nc.vector.tensor_scalar(row_i[:, :], t_row[:, :], float(E * REGION), None, ALU.min)
            nc.vector.tensor_scalar(expert_i[:, :], tile_e[:, :], float(E - 1), None,
                                    ALU.min).then_inc(table_ready, 1)
            dve.wait_ge(table_ready, 1)
            dve.wait_ge(moe_w, MOE_WEIGHTS)

            def step(at):
                if (t := at(0)):
                    e = dve.value_load(expert_i[0:1, bass.ds(t.n, 1)], min_val=0, max_val=E - 1)
                    dve.wait_ge(up_done, t.n + 1)
                    after(dve, ht_done, t.n - 1)
                    nc.vector.tensor_tensor(hb[t.slot % 2][:, :], up_bank[t.slot % 2][:, :],
                                            b1_sb[:, bass.ds(e * FF, FF)], ALU.add).then_inc(hb_ready, 1)
                if (t := at(2)):
                    dve.wait_ge(down_done, t.n + 1)
                    dve.wait_ge(x2b_ready, t.n + 1)
                    after(dve, y_out[t.slot], 16 * t.lap)
                    nc.vector.tensor_tensor(y_sb[t.slot][:, :], down_bank[t.slot % 2][:, 0:D],
                                            x2b[t.slot % 2][:, :], ALU.add).then_inc(y_ready, 1)

            steps(dve, step)

        @block.tensor
        def _(pe):
            def mm(o, l, r, start=True, stop=True):
                return nc.tensor.matmul(o, lhsT=l, rhs=r, start=start, stop=stop)

            def transpose(o, i):
                return nc.tensor.transpose(o, i, ident[:, :])

            def score(b, g):
                if g == 0:
                    pe.wait_ge(stack_in[b.slot], 16 * 2 * SLOTS * (b.lap + 1))
                qs, ks = stack[0][b.slot], stack[1][b.slot]
                for k, (kt, qt) in enumerate(((0, 0), (0, 1), (1, 1))):
                    after(pe, squared, 12 * b.n + 3 * (g - 1) + k + 1)
                    for c in range(GH):
                        h = HG * (g // 2) + 2 * c + g % 2
                        last = mm(score_bank[k][:, c * P:(c + 1) * P], ks[:, h, kt * P:(kt + 1) * P],
                                  qs[:, h, qt * P:(qt + 1) * P])
                    last.then_inc(scored, 1)

            def weigh(b, g):
                gg, r = g // 2, g % 2
                pe.wait_ge(masked, 8 * b.n + 2 * g + 2)
                if g == 0:
                    pe.wait_ge(v_ready, b.n + 1)
                if r == 0:
                    after(pe, u_ready, 2 * (b.n - 1) + gg + 1)
                    if gg == 1:
                        after(pe, prefix_read, b.n - 2)
                v = v_ext[b.slot]
                for c in range(GH):
                    mm(av_bank[gg][STRIP * c:STRIP * (c + 1), 0:L], v[:, 0, r, GH * gg + c, :],
                       scores[g][:, 0:2, c, :], start=r == 0, stop=False)
                for c in range(GH):
                    last = mm(av_bank[gg][STRIP * c:STRIP * (c + 1), P:L], v[:, 1, r, GH * gg + c, :],
                              scores[g][:, 2, c, :], start=False, stop=r == 1)
                last.then_inc(av_done, 1)

            def transpose_u(b):
                pe.wait_ge(u_ready, 2 * b.n + 2)
                after(pe, rest_ready[1], upto(b.n + 4))
                after(pe, v_ready, upto(b.n + 2))
                for g in range(NG):
                    for j in range(NTK):
                        c = j * NG + g
                        last = transpose(p5[:, c * P:(c + 1) * P], u_sb[g][:, j * P:(j + 1) * P])
                last.then_inc(tu_done, 1)

            def transpose_xn(b):
                pe.wait_ge(xn_ready, b.n + 1)
                after(pe, x2nT_ready, b.n - 4)
                after(pe, rest_ready[0], b.n)
                for j in range(NTK):
                    last = transpose(p6[:, j * P:(j + 1) * P], xn[:, j, :])
                last.then_inc(tn_done, 1)

            def project(b, o):
                pe.wait_ge(xnT_ready, b.n + 1)
                if o == 1:
                    after(pe, v_ready, b.n - 1)
                for g in range(NG):
                    last = mm((p6, p5)[o][:, g * L:(g + 1) * L], (wq_sb, wk_sb)[o][:, g * P:(g + 1) * P],
                              xnT[b.slot][:, :])
                last.then_inc(proj_done[o], 1)

            def project_v(b):
                after(pe, o_ready, b.n - 1)
                after(pe, rest_ready[1], upto(b.n + 2))
                for j in range(NTK):
                    last = mm(p5[:, j * P:(j + 1) * P], xnT[b.slot][:, j * P:(j + 1) * P], wv_sb[:, :])
                last.then_inc(v_done, 1)

            def transpose_o(b):
                pe.wait_ge(o_ready, b.n + 1)
                after(pe, logit_ready, b.n)
                for j in range(NTK):
                    last = transpose(p7[:, j * P:(j + 1) * P], o_sb[:, j, :, :].rearrange("p g n -> p (g n)"))
                last.then_inc(to_done, 1)

            def project_o(b):
                pe.wait_ge(oT_ready, b.n + 1)
                for j in range(NTK):
                    last = mm(p7[:, j * P:(j + 1) * P], oT[:, j * P:(j + 1) * P], wo_sb[:, :])
                last.then_inc(wo_done, 1)

            def transpose_x2n(b):
                pe.wait_ge(x2n_ready, b.n + 1)
                after(pe, rest_ready[0], upto(b.n + 5))
                for j in range(NTK):
                    last = transpose(p6[:, j * P:(j + 1) * P], x2n[b.slot][:, j, :])
                last.then_inc(tx_done, 1)

            def gate(b):
                pe.wait_ge(x2nT_ready, b.n + 1)
                for j in range(NTK):
                    last = mm(p7[:, j * E:(j + 1) * E], x2nT[:, j * P:(j + 1) * P], gw_sb[:, :])
                last.then_inc(gate_done, 1)

            def prefix(b):
                pe.wait_ge(onehot_ready, b.n + 1)
                after(pe, u_ready, upto(b.n + 3) * 2)
                mm(prefix_bank[:, 0:E], before[:, :], onehot[:, 0, :])
                mm(prefix_bank[:, E:2 * E], before[:, :], onehot[:, 1, :], stop=False)
                mm(prefix_bank[:, E:2 * E], ones[:, :], onehot[:, 0, :], start=False)
                mm(prefix_bank[:, 2 * E:3 * E], ones[:, :], onehot[:, 0, :], stop=False)
                mm(prefix_bank[:, 2 * E:3 * E], ones[:, :], onehot[:, 1, :], start=False).then_inc(prefix_done, 1)

            pe.wait_ge(pool_const, 2)
            pe.wait_ge(attn_w, ATTN_WEIGHTS)

            def period(at):
                new, vb, core, late, tail, route, nxt = at(0), at(1), at(2), at(3), at(4), at(5), at(-1)
                if core:
                    score(core, 0)
                if late:
                    weigh(late, 2)
                if tail:
                    project_o(tail)
                if new:
                    project(new, 0)
                if core:
                    score(core, 1)
                if late:
                    weigh(late, 3)
                if new:
                    project(new, 1)
                if core:
                    score(core, 2)
                    weigh(core, 0)
                if late:
                    transpose_u(late)
                if tail:
                    transpose_x2n(tail)
                if core:
                    score(core, 3)
                if route:
                    prefix(route)
                if core:
                    weigh(core, 1)
                if tail:
                    gate(tail)
                if vb:
                    project_v(vb)
                if nxt:
                    transpose_xn(nxt)
                if late:
                    transpose_o(late)

            periods(pe, period)
            pe.wait_ge(moe_w, MOE_WEIGHTS)
            pe.wait_ge(table_ready, 1)

            experts = [None] * RING

            def transpose_xw(t):
                pe.wait_ge(xr_in[t.slot], 16 * (t.lap + 1))
                after(pe, xwT_ready, t.n)
                transpose(xw_bank[:, 0:P], xr[t.slot][:, 0:D]).then_inc(xwt_done, 1)

            def expert_of(t):
                return pe.value_load(expert_i[0:1, bass.ds(t.n, 1)], min_val=0, max_val=E - 1)

            def go_up(t, e):
                pe.wait_ge(xwT_ready, t.n + 1)
                after(pe, hb_ready, t.n - 1)
                mm(up_bank[t.slot % 2][:, :], xwT[t.slot % 2][:, :],
                   w1_sb[:, bass.ds(e * FF, FF)]).then_inc(up_done, 1)

            def transpose_h(t):
                pe.wait_ge(hb_ready, t.n + 1)
                after(pe, hT_ready, t.n - 1)
                for c in range(FC):
                    last = transpose(hT_bank[t.slot % 2][:, c * P:(c + 1) * P], hb[t.slot % 2][:, c * P:(c + 1) * P])
                last.then_inc(ht_done, 1)

            def go_down(t, e):
                pe.wait_ge(hT_ready, t.n + 1)
                after(pe, y_ready, t.n - 1)
                for c in range(FC):
                    last = mm(down_bank[t.slot % 2][:, 0:D], hT[t.slot % 2][:, c * P:(c + 1) * P],
                              w2_sb[:, bass.ds(e * (FC * D) + c * D, D)], start=c == 0, stop=c == FC - 1)
                last.then_inc(down_done, 1)

            def step(at):
                if (t := at(0)):
                    experts[t.slot] = expert_of(t)
                    go_up(t, experts[t.slot])
                if (t := at(-1)):
                    transpose_xw(t)
                if (t := at(1)):
                    transpose_h(t)
                if (t := at(2)):
                    go_down(t, experts[t.slot] if at(0) and at(0).slot >= 2 else expert_of(t))

            transpose_xw(turn(0, RING, TILES))
            steps(pe, step)


_INS = ['L0_attn_hidden_states', 'L0_attn_Wq', 'L0_attn_Wk', 'L0_attn_Wv', 'L0_attn_Wo', 'L0_ffn_gate_w',
        'L0_ffn_gate_b', 'L0_ffn_w1', 'L0_ffn_b1', 'L0_ffn_w2', 'L0_ffn_b2']


def kernel(**inputs):
    import numpy as _np
    import concourse.bacc as _bacc
    from concourse import mybir as _mybir
    from concourse.bass_utils import run_bass_kernel_spmd as _run

    nc = _bacc.Bacc("TRN2", target_bir_lowering=False, num_devices=1)
    arrays, args = {}, []
    for name in _INS:
        a = _np.ascontiguousarray(inputs[name])
        arrays[f"in_{name}"] = a
        args.append(nc.dram_tensor(f"in_{name}", a.shape, _mybir.dt.from_np(a.dtype), kind="ExternalInput").ap())
    shape = inputs[_INS[0]].shape
    args.append(nc.dram_tensor("out_0", shape, _mybir.dt.float32, kind="ExternalOutput").ap())
    attention_moe_kernel(nc, *args)
    r = _run(nc, [arrays], core_ids=[0])
    return r.results[0]["out_0"]
```
